# Optimizing a Trainium2 kernel written in Bass

```python
import numpy as np
import jax
import jax.numpy as jnp

def _softmax(x, axis=-1):
    return jax.nn.softmax(x, axis=axis)

def _gelu(x):
    return jax.nn.gelu(x, approximate=True)

def _silu(x):
    return jax.nn.silu(x)

def _sigmoid(x):
    return jax.nn.sigmoid(x)

def _layernorm(x, axis=-1, eps=1e-05):
    m = jnp.mean(x, axis=axis, keepdims=True)
    v = jnp.var(x, axis=axis, keepdims=True)
    return (x - m) / jnp.sqrt(v + eps)

def _scatter_add(tgt, idx, src, axis=0):
    return tgt.at[idx].add(src)

def _segment_sum(src, seg, n):
    return jax.ops.segment_sum(src, seg, n)
kernel_name = 'mk_decoder_postln_d2_seqx_r8_b21ea7'

def setup_inputs(seed: int=0):
    np.random.seed(seed)
    _w = jnp.asarray

    def _rec_inputs():
        import jax
        import jax.numpy as jnp
        _rk = jax.random.key(seed)
        x = -0.0002928 + 1 * jax.random.normal(jax.random.fold_in(_rk, 1), (8, 128, 128), jnp.float32)
        _lenS = 128 - jax.random.randint(jax.random.fold_in(_rk, 7), (8,), 0, max(1, 128 // 4) + 1, jnp.int32)
        _lenS2 = 128 - jax.random.randint(jax.random.fold_in(_rk, 8), (8,), 0, max(1, 128 // 4) + 1, jnp.int32)
        _ctx_1024P = jax.random.normal(jax.random.fold_in(_rk, 11), (8, 16, 128), jnp.float32)
        _ctx_1024c = jax.random.dirichlet(jax.random.fold_in(_rk, 511), 0.3 * jnp.ones((16,), jnp.float32), (8, 128))
        _ctx_1024t = jnp.einsum('bsk,bkd->bsd', _ctx_1024c, _ctx_1024P)
        _ctx_1024t = _ctx_1024t * jax.lax.rsqrt(jnp.mean(jnp.square(_ctx_1024t)) + 1e-12) * 0.953939
        ctx_1024 = -1.39393e-06 + 0.999914 * (_ctx_1024t + 0.3 * jax.random.normal(jax.random.fold_in(_rk, 611), (8, 128, 128), jnp.float32))
        fside_BxSxS2_0 = jax.random.uniform(jax.random.fold_in(_rk, 12), (8, 128, 128), jnp.float32, 0.0, 1)
        _validS = jnp.arange(128)[None, :] < _lenS[:, None]
        _validS2 = jnp.arange(128)[None, :] < _lenS2[:, None]
        _causal = jnp.tril(jnp.ones((128, 128), dtype=bool))
        mask_BxSxS2_ik1 = jnp.where(jnp.broadcast_to(_validS2[:, None, :], (8, 128, 128)), 1, 0).astype(jnp.int32)
        return (x, ctx_1024, fside_BxSxS2_0, mask_BxSxS2_ik1)
    x, ctx_1024, fside_BxSxS2_0, mask_BxSxS2_ik1 = _rec_inputs()

    def _L0_attn_setup():
        import jax, jax.numpy as jnp
        import numpy as np
        N_EMBD = 128
        N_HEAD = 16
        D_K = N_EMBD // N_HEAD
        B, T = (2, 256)
        NEG = -10000000000.0
        key = jax.random.key(seed)
        ks = jax.random.split(key, 9)
        s = 1.0 / np.sqrt(N_EMBD)
        mk = lambda k: jax.random.uniform(k, (N_EMBD, N_EMBD), jnp.float32, -s, s)
        mb = lambda k: jax.random.uniform(k, (N_EMBD,), jnp.float32, -s, s)
        return {'x': jax.random.normal(ks[0], (B, T, N_EMBD), jnp.float32), 'Wq': mk(ks[1]), 'bq': mb(ks[2]), 'Wk': mk(ks[3]), 'bk': mb(ks[4]), 'Wv': mk(ks[5]), 'bv': mb(ks[6]), 'Wo': mk(ks[7]), 'bo': mb(ks[8])}
    _L0_attn_all = _L0_attn_setup()
    _L0_attn_in = {k: v for k, v in _L0_attn_all.items() if k in ('Wq', 'bq', 'Wk', 'bk', 'Wv', 'bv', 'Wo', 'bo')}
    del _L0_attn_all

    def _L0_xattn_setup():
        import jax, jax.numpy as jnp
        import numpy as np
        NUM_HEADS = 16
        HIDDEN = 128
        B, S = (2, 256)

        def _split_heads(x, H):
            b, s, d = x.shape
            return x.reshape(b, s, H, d // H).transpose(0, 2, 1, 3)
        key = jax.random.key(seed)
        ks = jax.random.split(key, 14)
        D = HIDDEN
        scale = 1.0 / np.sqrt(D)
        inp = {'query': jax.random.normal(ks[0], (B, S, D), jnp.float32), 'key_in': jax.random.normal(ks[1], (B, S, D), jnp.float32), 'value': jax.random.normal(ks[2], (B, S, D), jnp.float32), 'group_prob': jax.random.uniform(ks[3], (B, S, S), jnp.float32), 'mask': jax.random.randint(ks[4], (B, S, S), 0, 2, jnp.int32), 'wq_k': jax.random.normal(ks[5], (D, D), jnp.float32) * scale, 'wq_b': jnp.zeros((D,), jnp.float32), 'wk_k': jax.random.normal(ks[6], (D, D), jnp.float32) * scale, 'wk_b': jnp.zeros((D,), jnp.float32), 'wv_k': jax.random.normal(ks[7], (D, D), jnp.float32) * scale, 'wv_b': jnp.zeros((D,), jnp.float32), 'wo_k': jax.random.normal(ks[8], (D, D), jnp.float32) * scale, 'wo_b': jnp.zeros((D,), jnp.float32)}
        return inp
    _L0_xattn_all = _L0_xattn_setup()
    _L0_xattn_in = {k: v for k, v in _L0_xattn_all.items() if k in ('wq_k', 'wq_b', 'wk_k', 'wk_b', 'wv_k', 'wv_b', 'wo_k', 'wo_b')}
    del _L0_xattn_all

    def _L0_ffn_setup():
        import jax, jax.numpy as jnp
        import numpy as np
        B, S, D, O, E, R, TOP_K = (4, 128, 128, 128, 8, 16, 2)
        SCALING = 32.0 / 16.0
        NEG_INF = -1000000000.0
        key = jax.random.key(seed)
        ks = jax.random.split(key, 6)
        return {'x': jax.random.normal(ks[0], (B, S, D), jnp.float32), 'base_w': jax.random.normal(ks[1], (O, D), jnp.float32) * 0.02, 'base_b': jnp.zeros((O,), jnp.float32), 'lora_A': jax.random.normal(ks[2], (E, D, R), jnp.float32) * 0.02, 'lora_B': jax.random.normal(ks[3], (E, R, O), jnp.float32) * 0.02, 'router_w': jax.random.normal(ks[4], (E, D), jnp.float32) * 0.02, 'router_b': jnp.zeros((E,), jnp.float32)}
    _L0_ffn_all = _L0_ffn_setup()
    _L0_ffn_in = {k: v for k, v in _L0_ffn_all.items() if k in ('base_w', 'base_b', 'lora_A', 'lora_B', 'router_w', 'router_b')}
    del _L0_ffn_all

    def _L1_attn_setup():
        import jax, jax.numpy as jnp
        import numpy as np
        B, T, D_IN, D_PROJ, D_OUT, MEM = (8, 256, 128, 128, 128, 40)

        def _fsmn_memory(p, memory_weights):
            M = memory_weights.shape[0] - 1
            b, t, d = p.shape
            rhs = memory_weights[1:][::-1].T[:, None, :]
            lhs = jnp.pad(p.transpose(0, 2, 1), ((0, 0), (0, 0), (M - 1, 0)))
            band = jax.lax.conv_general_dilated(lhs, rhs, window_strides=(1,), padding='VALID', feature_group_count=d, dimension_numbers=('NCH', 'OIH', 'NCH')).transpose(0, 2, 1)
            cs = jnp.cumsum(p, axis=1)
            band_sum = cs - jnp.pad(cs, ((0, 0), (M, 0), (0, 0)))[:, :t]
            total = cs[:, -1:]
            return band + memory_weights[0] * (total - band_sum)
        key = jax.random.key(seed)
        k1, k2, k3, k4 = jax.random.split(key, 4)
        x = jax.random.normal(k1, (B, T, D_IN), dtype=jnp.float32)
        lim1 = np.sqrt(6.0 / (D_IN + D_PROJ))
        lim2 = np.sqrt(6.0 / (D_PROJ + D_OUT))
        limm = np.sqrt(6.0 / (MEM + 1 + D_PROJ))
        W1 = jax.random.uniform(k2, (D_IN, D_PROJ), minval=-lim1, maxval=lim1, dtype=jnp.float32)
        W2 = jax.random.uniform(k3, (D_PROJ, D_OUT), minval=-lim2, maxval=lim2, dtype=jnp.float32)
        mw = jax.random.uniform(k4, (MEM + 1, D_PROJ), minval=-limm, maxval=limm, dtype=jnp.float32)
        mw = mw.at[0].set(0.0)
        bias1 = jnp.ones((D_PROJ,), dtype=jnp.float32)
        bias2 = jnp.ones((D_OUT,), dtype=jnp.float32)
        return {'input_data': x, 'W1': W1, 'bias1': bias1, 'W2': W2, 'bias2': bias2, 'memory_weights': mw}
    _L1_attn_all = _L1_attn_setup()
    _L1_attn_in = {k: v for k, v in _L1_attn_all.items() if k in ('W1', 'bias1', 'W2', 'bias2', 'memory_weights')}
    del _L1_attn_all

    def _L1_xattn_setup():
        import jax, jax.numpy as jnp
        import numpy as np
        SCALE_BASE = 512.0
        GN_EPS = 1e-05

        def _xpos(x, downscale):
            L, D = (x.shape[-2], x.shape[-1])
            half = D // 2
            base = (jnp.arange(0, D, 2, dtype=jnp.float32) + 0.4 * D) / (1.4 * D)
            min_pos = -(L // 2)
            power = (jnp.arange(min_pos, min_pos + L, dtype=jnp.float32) / SCALE_BASE)[:, None]
            scale = base[None, :] ** power
            inv_freq = 1.0 / 10000.0 ** (jnp.arange(half, dtype=jnp.float32) / half)
            ang = jnp.arange(L, dtype=jnp.float32)[:, None] * inv_freq[None, :]
            sin, cos = (jnp.sin(ang), jnp.cos(ang))
            if downscale:
                scale = 1.0 / scale
            sin_s = jnp.repeat(sin * scale, 2, axis=-1)
            cos_s = jnp.repeat(cos * scale, 2, axis=-1)
            x1, x2 = (x[..., ::2], x[..., 1::2])
            rot = jnp.stack((-x2, x1), axis=-1).reshape(x.shape)
            return x * cos_s + rot * sin_s

        def _decay_mask(L, H):
            gammas = 1.0 - jnp.exp(jnp.linspace(np.log(1.0 / 32.0), np.log(1.0 / 512.0), H)).astype(jnp.float32)
            idx = jnp.arange(L)
            dist = idx[:, None] - idx[None, :]
            causal = dist >= 0
            d = jnp.maximum(dist, 0).astype(jnp.float32)
            return jnp.where(causal[None], gammas[:, None, None] ** d[None], 0.0)
        key = jax.random.key(seed)
        ks = jax.random.split(key, 9)
        B, L, D, H = (2, 256, 128, 16)
        hd = D // H
        return {'query': jax.random.normal(ks[0], (B, L, D), jnp.float32), 'key': jax.random.normal(ks[1], (B, L, D), jnp.float32), 'value': jax.random.normal(ks[2], (B, L, D), jnp.float32), 'W_Q': jax.random.normal(ks[3], (H, D, hd), jnp.float32) / D, 'W_K': jax.random.normal(ks[4], (H, D, hd), jnp.float32) / D, 'W_V': jax.random.normal(ks[5], (H, D, hd), jnp.float32) / D, 'g_w': jax.random.normal(ks[6], (D, D), jnp.float32) * (2.0 / (D + D)) ** 0.5, 'g_b': jnp.zeros((D,), jnp.float32), 'out_w': jax.random.normal(ks[7], (D, D), jnp.float32) * (2.0 / (D + D)) ** 0.5, 'out_b': jnp.zeros((D,), jnp.float32)}
    _L1_xattn_all = _L1_xattn_setup()
    _L1_xattn_in = {k: v for k, v in _L1_xattn_all.items() if k in ('W_Q', 'W_K', 'W_V', 'g_w', 'g_b', 'out_w', 'out_b')}
    del _L1_xattn_all

    def _L1_ffn_setup():
        import jax, jax.numpy as jnp
        import numpy as np
        D_IN, D_HID = (128, 512)

        def _ternary(key, shape):
            return jax.random.randint(key, shape, -1, 2).astype(jnp.float32)

        def _tlin(x, w, s):
            return jnp.einsum('bsi,oi->bso', x, w) * s
        key = jax.random.key(seed)
        ks = jax.random.split(key, 12)
        inv = lambda fan: 1.0 / np.sqrt(fan).astype(np.float32)
        return {'x': jax.random.normal(ks[0], (4, 256, D_IN), dtype=jnp.float32), 'w1_w': _ternary(ks[1], (D_HID, D_IN)), 'w1_s': jax.random.uniform(ks[2], (D_HID,), dtype=jnp.float32) * inv(D_IN), 'w2_w': _ternary(ks[3], (D_HID, D_IN)), 'w2_s': jax.random.uniform(ks[4], (D_HID,), dtype=jnp.float32) * inv(D_IN), 'h1_w': _ternary(ks[5], (D_HID, D_HID)), 'h1_s': jax.random.uniform(ks[6], (D_HID,), dtype=jnp.float32) * inv(D_HID), 'h2_w': _ternary(ks[7], (D_HID, D_HID)), 'h2_s': jax.random.uniform(ks[8], (D_HID,), dtype=jnp.float32) * inv(D_HID), 'w3_w': _ternary(ks[9], (D_IN, D_HID)), 'w3_s': jax.random.uniform(ks[10], (D_IN,), dtype=jnp.float32) * inv(D_HID)}
    _L1_ffn_all = _L1_ffn_setup()
    _L1_ffn_in = {k: v for k, v in _L1_ffn_all.items() if k in ('w1_w', 'w1_s', 'w2_w', 'w2_s', 'h1_w', 'h1_s', 'h2_w', 'h2_s', 'w3_w', 'w3_s')}
    del _L1_ffn_all
    return {'x': x, 'ctx_1024': ctx_1024, 'fside_BxSxS2_0': fside_BxSxS2_0, 'mask_BxSxS2_ik1': mask_BxSxS2_ik1, 'L0_attn_Wq': _L0_attn_in['Wq'], 'L0_attn_bq': _L0_attn_in['bq'], 'L0_attn_Wk': _L0_attn_in['Wk'], 'L0_attn_bk': _L0_attn_in['bk'], 'L0_attn_Wv': _L0_attn_in['Wv'], 'L0_attn_bv': _L0_attn_in['bv'], 'L0_attn_Wo': _L0_attn_in['Wo'], 'L0_attn_bo': _L0_attn_in['bo'], 'L0_xattn_wq_k': _L0_xattn_in['wq_k'], 'L0_xattn_wq_b': _L0_xattn_in['wq_b'], 'L0_xattn_wk_k': _L0_xattn_in['wk_k'], 'L0_xattn_wk_b': _L0_xattn_in['wk_b'], 'L0_xattn_wv_k': _L0_xattn_in['wv_k'], 'L0_xattn_wv_b': _L0_xattn_in['wv_b'], 'L0_xattn_wo_k': _L0_xattn_in['wo_k'], 'L0_xattn_wo_b': _L0_xattn_in['wo_b'], 'L0_ffn_base_w': _L0_ffn_in['base_w'], 'L0_ffn_base_b': _L0_ffn_in['base_b'], 'L0_ffn_lora_A': _L0_ffn_in['lora_A'], 'L0_ffn_lora_B': _L0_ffn_in['lora_B'], 'L0_ffn_router_w': _L0_ffn_in['router_w'], 'L0_ffn_router_b': _L0_ffn_in['router_b'], 'L1_attn_W1': _L1_attn_in['W1'], 'L1_attn_bias1': _L1_attn_in['bias1'], 'L1_attn_W2': _L1_attn_in['W2'], 'L1_attn_bias2': _L1_attn_in['bias2'], 'L1_attn_memory_weights': _L1_attn_in['memory_weights'], 'L1_xattn_W_Q': _L1_xattn_in['W_Q'], 'L1_xattn_W_K': _L1_xattn_in['W_K'], 'L1_xattn_W_V': _L1_xattn_in['W_V'], 'L1_xattn_g_w': _L1_xattn_in['g_w'], 'L1_xattn_g_b': _L1_xattn_in['g_b'], 'L1_xattn_out_w': _L1_xattn_in['out_w'], 'L1_xattn_out_b': _L1_xattn_in['out_b'], 'L1_ffn_w1_w': _L1_ffn_in['w1_w'], 'L1_ffn_w1_s': _L1_ffn_in['w1_s'], 'L1_ffn_w2_w': _L1_ffn_in['w2_w'], 'L1_ffn_w2_s': _L1_ffn_in['w2_s'], 'L1_ffn_h1_w': _L1_ffn_in['h1_w'], 'L1_ffn_h1_s': _L1_ffn_in['h1_s'], 'L1_ffn_h2_w': _L1_ffn_in['h2_w'], 'L1_ffn_h2_s': _L1_ffn_in['h2_s'], 'L1_ffn_w3_w': _L1_ffn_in['w3_w'], 'L1_ffn_w3_s': _L1_ffn_in['w3_s']}

def reference(x, ctx_1024, fside_BxSxS2_0, mask_BxSxS2_ik1, L0_attn_Wq, L0_attn_bq, L0_attn_Wk, L0_attn_bk, L0_attn_Wv, L0_attn_bv, L0_attn_Wo, L0_attn_bo, L0_xattn_wq_k, L0_xattn_wq_b, L0_xattn_wk_k, L0_xattn_wk_b, L0_xattn_wv_k, L0_xattn_wv_b, L0_xattn_wo_k, L0_xattn_wo_b, L0_ffn_base_w, L0_ffn_base_b, L0_ffn_lora_A, L0_ffn_lora_B, L0_ffn_router_w, L0_ffn_router_b, L1_attn_W1, L1_attn_bias1, L1_attn_W2, L1_attn_bias2, L1_attn_memory_weights, L1_xattn_W_Q, L1_xattn_W_K, L1_xattn_W_V, L1_xattn_g_w, L1_xattn_g_b, L1_xattn_out_w, L1_xattn_out_b, L1_ffn_w1_w, L1_ffn_w1_s, L1_ffn_w2_w, L1_ffn_w2_s, L1_ffn_h1_w, L1_ffn_h1_s, L1_ffn_h2_w, L1_ffn_h2_s, L1_ffn_w3_w, L1_ffn_w3_s):
    import jax
    import jax.numpy as jnp

    def _L0_attn_ref(x, Wq, bq, Wk, bk, Wv, bv, Wo, bo):
        import jax, jax.numpy as jnp
        import numpy as np
        N_EMBD = 128
        N_HEAD = 16
        D_K = N_EMBD // N_HEAD
        B, T = (2, 256)
        NEG = -10000000000.0
        Bx, Tx, _ = x.shape
        split = lambda h: h.reshape(Bx, Tx, N_HEAD, D_K).transpose(0, 2, 1, 3)
        q = split(x @ Wq.T + bq)
        k = split(x @ Wk.T + bk)
        v = split(x @ Wv.T + bv)
        scores = jnp.einsum('bhqd,bhkd->bhqk', q, k) / np.sqrt(D_K)
        causal = jnp.tril(jnp.ones((Tx, Tx), dtype=bool))
        scores = jnp.where(causal[None, None], scores, NEG)
        prob = jax.nn.softmax(scores, axis=-1)
        y = jnp.einsum('bhqk,bhkd->bhqd', prob, v)
        y = y.transpose(0, 2, 1, 3).reshape(Bx, Tx, N_EMBD)
        return y @ Wo.T + bo

    def _L0_xattn_ref(query, key_in, value, group_prob, mask, wq_k, wq_b, wk_k, wk_b, wv_k, wv_b, wo_k, wo_b):
        import jax, jax.numpy as jnp
        import numpy as np
        NUM_HEADS = 16
        HIDDEN = 128
        B, S = (2, 256)

        def _split_heads(x, H):
            b, s, d = x.shape
            return x.reshape(b, s, H, d // H).transpose(0, 2, 1, 3)
        H = NUM_HEADS
        dh = query.shape[-1] // H
        q = _split_heads(query @ wq_k + wq_b, H)
        k = _split_heads(key_in @ wk_k + wk_b, H)
        v = _split_heads(value @ wv_k + wv_b, H)
        logits = jnp.einsum('bhqd,bhkd->bhqk', q, k) / jnp.sqrt(jnp.asarray(dh, q.dtype))
        neg = (1.0 - mask.astype(q.dtype)) * -1000000000.0
        logits = logits + neg[:, None, :, :]
        attn = jax.nn.softmax(logits, axis=-1)
        attn = attn * group_prob[:, None, :, :]
        out = jnp.einsum('bhqk,bhkd->bhqd', attn, v)
        out = out.transpose(0, 2, 1, 3).reshape(query.shape[0], -1, H * dh)
        return out @ wo_k + wo_b

    def _L0_ffn_ref(x, base_w, base_b, lora_A, lora_B, router_w, router_b):
        import jax, jax.numpy as jnp
        import numpy as np
        B, S, D, O, E, R, TOP_K = (4, 128, 128, 128, 8, 16, 2)
        SCALING = 32.0 / 16.0
        NEG_INF = -1000000000.0
        result = jnp.einsum('bsd,od->bso', x, base_w) + base_b
        ax = jnp.einsum('bsd,edr->bser', x, lora_A)
        bax = jnp.einsum('bser,ero->bseo', ax, lora_B)
        logits = jnp.einsum('bsd,ed->bse', x, router_w) + router_b
        kth = jax.lax.top_k(logits, TOP_K)[0][..., -1:]
        masked = jnp.where(logits < kth, NEG_INF, logits)
        expert_weights = jax.nn.softmax(masked, axis=-1)
        return result + SCALING * jnp.einsum('bse,bseo->bso', expert_weights, bax)

    def _L1_attn_ref(input_data, W1, bias1, W2, bias2, memory_weights):
        import jax, jax.numpy as jnp
        import numpy as np
        B, T, D_IN, D_PROJ, D_OUT, MEM = (8, 256, 128, 128, 128, 40)

        def _fsmn_memory(p, memory_weights):
            M = memory_weights.shape[0] - 1
            b, t, d = p.shape
            rhs = memory_weights[1:][::-1].T[:, None, :]
            lhs = jnp.pad(p.transpose(0, 2, 1), ((0, 0), (0, 0), (M - 1, 0)))
            band = jax.lax.conv_general_dilated(lhs, rhs, window_strides=(1,), padding='VALID', feature_group_count=d, dimension_numbers=('NCH', 'OIH', 'NCH')).transpose(0, 2, 1)
            cs = jnp.cumsum(p, axis=1)
            band_sum = cs - jnp.pad(cs, ((0, 0), (M, 0), (0, 0)))[:, :t]
            total = cs[:, -1:]
            return band + memory_weights[0] * (total - band_sum)
        p = jnp.matmul(input_data, W1) + bias1
        p = _fsmn_memory(p, memory_weights)
        return jnp.matmul(p, W2) + bias2

    def _L1_xattn_ref(query, key, value, W_Q, W_K, W_V, g_w, g_b, out_w, out_b):
        import jax, jax.numpy as jnp
        import numpy as np
        SCALE_BASE = 512.0
        GN_EPS = 1e-05

        def _xpos(x, downscale):
            L, D = (x.shape[-2], x.shape[-1])
            half = D // 2
            base = (jnp.arange(0, D, 2, dtype=jnp.float32) + 0.4 * D) / (1.4 * D)
            min_pos = -(L // 2)
            power = (jnp.arange(min_pos, min_pos + L, dtype=jnp.float32) / SCALE_BASE)[:, None]
            scale = base[None, :] ** power
            inv_freq = 1.0 / 10000.0 ** (jnp.arange(half, dtype=jnp.float32) / half)
            ang = jnp.arange(L, dtype=jnp.float32)[:, None] * inv_freq[None, :]
            sin, cos = (jnp.sin(ang), jnp.cos(ang))
            if downscale:
                scale = 1.0 / scale
            sin_s = jnp.repeat(sin * scale, 2, axis=-1)
            cos_s = jnp.repeat(cos * scale, 2, axis=-1)
            x1, x2 = (x[..., ::2], x[..., 1::2])
            rot = jnp.stack((-x2, x1), axis=-1).reshape(x.shape)
            return x * cos_s + rot * sin_s

        def _decay_mask(L, H):
            gammas = 1.0 - jnp.exp(jnp.linspace(np.log(1.0 / 32.0), np.log(1.0 / 512.0), H)).astype(jnp.float32)
            idx = jnp.arange(L)
            dist = idx[:, None] - idx[None, :]
            causal = dist >= 0
            d = jnp.maximum(dist, 0).astype(jnp.float32)
            return jnp.where(causal[None], gammas[:, None, None] ** d[None], 0.0)
        B, L, D = query.shape
        H = W_Q.shape[0]
        q = jnp.einsum('bld,hde->bhle', query, W_Q)
        k = jnp.einsum('bld,hde->bhle', key, W_K)
        v = jnp.einsum('bld,hde->bhle', value, W_V)
        q = _xpos(q, downscale=False)
        k = _xpos(k, downscale=True)
        sim = jnp.einsum('bhnd,bhsd->bhns', q, k) * _decay_mask(L, H)[None]
        ret = jnp.einsum('bhns,bhsd->bhnd', sim, v)
        mu = ret.mean(axis=-1, keepdims=True)
        var = ret.var(axis=-1, keepdims=True)
        ret = (ret - mu) / jnp.sqrt(var + GN_EPS)
        ret = ret.transpose(0, 2, 1, 3).reshape(B, L, D)
        gate = jax.nn.silu(query @ g_w.T + g_b)
        return ret * gate @ out_w.T + out_b

    def _L1_ffn_ref(x, w1_w, w1_s, w2_w, w2_s, h1_w, h1_s, h2_w, h2_s, w3_w, w3_s):
        import jax, jax.numpy as jnp
        import numpy as np
        D_IN, D_HID = (128, 512)

        def _ternary(key, shape):
            return jax.random.randint(key, shape, -1, 2).astype(jnp.float32)

        def _tlin(x, w, s):
            return jnp.einsum('bsi,oi->bso', x, w) * s
        h = jax.nn.silu(_tlin(x, w1_w, w1_s)) * _tlin(x, w2_w, w2_s)
        h = jax.nn.gelu(_tlin(h, h1_w, h1_s), approximate=False)
        h = jax.nn.gelu(_tlin(h, h2_w, h2_s), approximate=False)
        return _tlin(h, w3_w, w3_s)
    x = _layernorm(x + _L0_attn_ref(x, L0_attn_Wq, L0_attn_bq, L0_attn_Wk, L0_attn_bk, L0_attn_Wv, L0_attn_bv, L0_attn_Wo, L0_attn_bo), axis=-1)
    x = _layernorm(x + _L0_xattn_ref(x, ctx_1024, ctx_1024, fside_BxSxS2_0, mask_BxSxS2_ik1, L0_xattn_wq_k, L0_xattn_wq_b, L0_xattn_wk_k, L0_xattn_wk_b, L0_xattn_wv_k, L0_xattn_wv_b, L0_xattn_wo_k, L0_xattn_wo_b), axis=-1)
    x = _layernorm(x + _L0_ffn_ref(x, L0_ffn_base_w, L0_ffn_base_b, L0_ffn_lora_A, L0_ffn_lora_B, L0_ffn_router_w, L0_ffn_router_b), axis=-1)
    x = _layernorm(x + _L1_attn_ref(x, L1_attn_W1, L1_attn_bias1, L1_attn_W2, L1_attn_bias2, L1_attn_memory_weights), axis=-1)
    x = _layernorm(x + _L1_xattn_ref(x, ctx_1024, ctx_1024, L1_xattn_W_Q, L1_xattn_W_K, L1_xattn_W_V, L1_xattn_g_w, L1_xattn_g_b, L1_xattn_out_w, L1_xattn_out_b), axis=-1)
    x = _layernorm(x + _L1_ffn_ref(x, L1_ffn_w1_w, L1_ffn_w1_s, L1_ffn_w2_w, L1_ffn_w2_s, L1_ffn_h1_w, L1_ffn_h1_s, L1_ffn_h2_w, L1_ffn_h2_s, L1_ffn_w3_w, L1_ffn_w3_s), axis=-1)
    return x

_drawn_inputs = setup_inputs


def setup_inputs(seed=0):
    import zlib

    import numpy as np

    out = dict(_drawn_inputs(seed))
    spreads = {'L0_xattn_wq_b': (0.0, 0.632),
     'L0_xattn_wk_b': (0.0, 0.8),
     'L0_xattn_wv_b': (0.0, 0.1),
     'L0_xattn_wo_b': (0.0, 0.1),
     'L0_ffn_base_b': (0.0, 0.1),
     'L0_ffn_router_b': (0.0, 0.561),
     'L1_attn_bias1': (1.0, 0.2),
     'L1_attn_bias2': (1.0, 0.2),
     'L1_xattn_g_b': (0.0, 0.1),
     'L1_xattn_out_b': (0.0, 0.1)}
    factors = {'L0_attn_bq': 8.0,
     'L0_attn_bk': 8.0,
     'L0_ffn_router_w': 2.688,
     'L1_ffn_w1_w': 8.0,
     'L1_ffn_w1_s': 8.0,
     'L1_ffn_w2_w': 8.0,
     'L1_ffn_w2_s': 8.0,
     'L1_ffn_h1_w': 8.0,
     'L1_ffn_h1_s': 8.0,
     'L1_ffn_h2_w': 8.0,
     'L1_ffn_h2_s': 8.0,
     'L1_ffn_w3_w': 8.0,
     'L1_ffn_w3_s': 8.0}
    for name, (base, spread) in spreads.items():
        noise = np.random.default_rng([zlib.crc32(name.encode()), seed]).standard_normal(out[name].shape)
        drawn = base * np.exp(spread * noise) if base else spread * noise
        out[name] = jnp.asarray(drawn.astype(out[name].dtype))
    for name, factor in factors.items():
        out[name] = (out[name] * factor).astype(out[name].dtype)
    return out
```

```python
from contextlib import ExitStack
import math

import concourse.bass as bass
from concourse import mybir
from concourse.alu_op_type import AluOpType as ALU

F32 = mybir.dt.float32
BF16 = mybir.dt.bfloat16
I32 = mybir.dt.int32
ACT = mybir.ActivationFunctionType
AX = mybir.AxisListType

B, S, D = 8, 128, 128
H, DH = 16, 8
PAIRS = B // 2
HG = 4
GROUPS = H // HG
UNITS = 2 * GROUPS
E_, R_ = 8, 16
TAPS = 40
POOL_TAPS = 10
PRODUCTS = 3
CHUNKS = 4
HID = 512
KT = HID // 128
EPS = 1e-5
SCALE = 1.0 / math.sqrt(DH)
MASK_DIAG, MASK_HI, MASK_LO = 64000.0, 15616.0, 9.0
A0, A1, RET = 0, 1, 2
CORE_STEPS = 3 * PAIRS

COLS = dict(bq0=0, bk0=1, bq1=2, bk1=3, bias1=4, gb=5, s1=6, s2=10, sh1=14, sh2=18, mw=22)
NCOLS = 22 + TAPS + 1
ROWS = dict(bv0=0, bo0=1, bv1=2, bo1=3, base_b=4, bias2=5, out_b=6, s3=7)


STEPS = [(A0, 0), (A0, 1), (A0, 2), (A1, 0), (A0, 3), (A1, 1), (A1, 2), (A1, 3), (RET, 0), (RET, 1), (RET, 2), (RET, 3)]
STEP_OF = {cp: k for k, cp in enumerate(STEPS)}
SOFTMAX_UNITS = 2 * PAIRS * UNITS
assert all((core == RET) == (k >= 2 * PAIRS) for k, (core, j) in enumerate(STEPS))


def unit(u):
    core, j = STEPS[u // UNITS]
    e, g = (u // GROUPS) % 2, u % GROUPS
    return core, 2 * j + e, g, e


def seq_no(core, b):
    return 2 * STEP_OF[core, b // 2] + b % 2


def make_schedule():
    at = {}

    def put(step, slot, *items):
        while slot >= UNITS:
            step, slot = step + 1, slot - UNITS
        at.setdefault((step, slot), []).extend(items)

    for k, (core, j) in enumerate(STEPS):
        if core == RET:
            put(k, 4, ("grab", 2 * j))
            put(k, 8, ("grab", 2 * j + 1))
            put(k, 9, ("center", j))
            put(k, 10, ("spread", j))
            put(k, 11, ("retY", j))
            put(k, 12, ("rstd", 4, j))
            put(k, 13, ("apply", 4, j))
            put(k, 14, ("xT", 4, j))
            continue
        for e in range(2):
            b = 2 * j + e
            put(k, 4 * e + 3, ("recip", core, b))
            put(k, 4 * e + 4, ("rT", core, b))
            put(k, 4 * e + 5, ("outT", core, b))
            put(k, 4 * e + 6, ("y", core, b))
        put(k, 11, ("rstd", core, j))
        put(k, 12, ("apply", core, j))
        put(k, 13, ("xT", core, j))
        if core == A0:
            put(k, 14, ("projQ1", j))
            put(STEP_OF[A0, j], 9, ("bd", A1, j))
            continue
        put(k, 14, ("route", j))
        put(k, 15, ("gate", j))
        put(k, 17, ("experts", j))
        put(k, 18, ("rstd", 2, j))
        put(k, 19, ("apply", 2, j))
        put(k, 20, ("xT", 2, j))
        put(k, 21, ("projP", j))
        for c in range(CHUNKS):
            put(k, 22 + c, ("taps", j, c))
        s = 22 + CHUNKS
        put(k, s, ("memY", j))
        put(k, s + 1, ("rstd", 3, j))
        put(k, s + 2, ("apply", 3, j))
        put(k, s + 3, ("xT", 3, j))
        put(k, s + 3, ("projQ4", j))
        put(k, s + 3, ("bd", RET, j))
        put(k, s + 4, ("silu", j))
    for h in range(2):
        put(0, 1 + h, ("projK", 1, h))
        put(0, 3 + h, ("projV", 1, h))
        put(1, 2 + h, ("projK4", h))
        put(1, 4 + h, ("projV", 2, h))
    for j, first in ((0, 8 * 10 + 1), (1, 8 * 11 + 2)):
        for n, item in enumerate(ffn_items(j)):
            put(0, first + n, item)
    slot = 8 * CORE_STEPS + 3
    for layer in range(3):
        for j in (2, 3):
            if (layer, j) == (0, 3):
                slot = max(slot, 8 * CORE_STEPS + 7)
            for item in ffn_items(j):
                if item[0] == "ff" and item[2] == layer:
                    put(0, slot, item)
                    slot += 1
    for j in (2, 3):
        put(0, slot, ("ffY", j))
        slot += 1
    for item, at_ in [(i, sl) for sl, its in at.items() for i in its if i[0] == "ffY"]:
        j = item[1]
        at[at_].append(("rstd", 5, j))
        put(at_[0], at_[1] + (1 if j < 3 else 0), ("apply", 5, j))
    return {place: sorted(items, key=lambda item: item[0] == "taps") for place, items in at.items()}


def ffn_items(j):
    return ([("ff", j, 0, m) for m in range(KT)] + [("ff", j, layer, m) for layer in (1, 2) for m in range(KT // 2)]
            + [("ffY", j)] * (j < 2))


PROLOGUE = [("projK", 0, 0), ("bd", A0, 0), ("projQ0", 0), ("bd", A0, 1), ("projV", 0, 0),
            ("projK", 0, 1), ("bd", A0, 2), ("bd", A0, 3), ("projQ0", 1), ("projV", 0, 1)]
MISC_USES = dict(rT=1, y=1, xT=1, projQ1=1, projK=1, projV=1, projK4=2, projQ0=1, route=1, experts=2,
                 projP=1, memY=1, projQ4=2, silu=1, center=1, spread=1, retY=1, ffY=1)
WALK_STEPS = CORE_STEPS + 5


def build(nc, t):
    schedule = make_schedule()
    order = [*PROLOGUE]
    for k in range(WALK_STEPS):
        for v in range(UNITS):
            order += schedule.get((k, v), [])
    misc_at, n = {}, 0
    for item in order:
        misc_at[item] = n
        n += MISC_USES.get(item[0], 0)
    n_misc = n

    with ExitStack() as ctx:
        def sb(name, shape, dt=F32):
            return ctx.enter_context(nc.sbuf_tensor(name, shape, dt))

        def sem(name):
            return ctx.enter_context(nc.semaphore(name))

        X = sb("X", [128, B, D])
        XB = sb("XB", [128, B, D])
        Z = sb("Z", [128, B, D])
        wh = sb("wh", [128, 2, KT, HID])
        early = wh[:, :, :, :].rearrange("p a b c -> p (a b c)")
        kT = early[:, 0:2 * B * S].rearrange("p (c n) -> p c n", c=2)
        maskI = early[:, 2 * B * S:3 * B * S].bitcast(I32).rearrange("p (b s) -> p b s", b=B)
        xT0 = early[:, 3 * B * S:4 * B * S]
        ctxT = sb("ctxT", [128, B * S])
        gT = sb("gT", [128, B, S])
        maskHi = sb("maskHi", [128, B, S], BF16)
        maskLo = sb("maskLo", [128, B, S], BF16)
        bd = sb("bd", [128, B, H, S])
        vpad = sb("vpad", [128, 2, H, D])
        vals = sb("vals", [128, 3, B, D])
        statT = sb("statT", [128, 3, B * S])
        stat = sb("stat", [128, 2, S])
        probs = sb("probs", [128, 2, HG * S])
        weightsT = sb("weightsT", [128, 3, HG, S])
        nmax = sb("nmax", [128, UNITS, HG])
        rowsum = sb("rowsum", [128, 2, H])
        recip = sb("recip", [128, 2, H])
        rexp = sb("rexp", [128, 2, H, DH])
        rTs = sb("rTs", [128, 2, S])
        outT = sb("outT", [128, 2, S])
        st6 = sb("st6", [128, 2, 6])
        mv = sb("mv", [128, 5, B, 2])
        nmean = sb("nmean", [128, 5, B])
        nmr = sb("nmr", [128, 5, B])
        vpe = sb("vpe", [128, 5, B])
        rstd = sb("rstd", [128, 5, B])
        mhalf = sb("mhalf", [128, 1])
        xTs = sb("xTs", [128, 4, 2 * S])
        lg = sb("lg", [128, 2, E_])
        top = sb("top", [128, 2, 8])
        lsub = sb("lsub", [128, 2, E_])
        lexp = sb("lexp", [128, 2, E_])
        keep = sb("keep", [128, 2, E_])
        kept = sb("kept", [128, 2, E_])
        esum = sb("esum", [128, 2])
        erec = sb("erec", [128, 2])
        wexp = sb("wexp", [128, 2, E_])
        gated = sb("gated", [128, 2, E_, R_])
        gatedT = sb("gatedT", [128, 2 * S])
        axs = sb("axs", [128, 2, E_, R_])
        PADW = TAPS - 1 + S
        pPad = sb("pPad", [128, 2, 2, PADW])
        psum_all = sb("psum_all", [128, 2, 2])
        ptot = sb("ptot", [128, 2, 2])
        mem = ctxT[:, 0:4 * S].rearrange("p (a b s) -> p a b s", a=2, b=2)
        memP = sb("memP", [128, 2, 2, S])
        prod = sb("prod", [128, PRODUCTS, 2, S])
        mwd = sb("mwd", [128, TAPS])
        qa = sb("qa", [128, 2, S])
        qb = sb("qb", [128, 2, S])
        q4T = statT[:, 1, :]
        silu = vals[:, 0, :, :].rearrange("p b d -> p (b d)")
        ret = sb("ret", [128, 2, 2 * S])
        cen = ctxT[:, 4 * S:8 * S].rearrange("p (a n) -> p a n", a=2)
        sq = sb("sq", [128, 2 * S])
        sd = sb("sd", [128, 2 * S])
        rsd = sb("rsd", [128, 2 * S])
        rg = sb("rg", [128, 2 * S])
        rg2 = sb("rg2", [128, 2 * S])
        causalT = sb("causalT", [128, S])
        bdw = bd[:, :, :, :].rearrange("p b h s -> p (b h s)")
        hid = [bdw[:, n * 2048:(n + 1) * 2048].rearrange("p (a m s) -> p a m s", a=2, m=KT) for n in range(3)]
        gateA = probs[:, :, 0:2 * S]
        ysc = sb("ysc", [128, 2, D])
        x5T = statT[:, 0, :].rearrange("p (j n) -> p j n", j=PAIRS)
        w0 = sb("w0", [128, 4, 128])
        w1 = sb("w1", [128, 4, 128])
        wr = sb("wr", [128, 7, 128])
        wm = sb("wm", [128, 2 * 128 + 128 + E_])
        wf = sb("wf", [128, 2, 128])
        wi = gT[:, :, :].rearrange("p b s -> p (b s)").rearrange("p (i n) -> p i n", i=2)
        wo3 = maskHi[:, :, :].rearrange("p b s -> p (b s)").bitcast(F32).rearrange("p (k n) -> p k n", k=KT)
        cols = sb("cols", [128, NCOLS])
        rows = sb("rows", [128, len(ROWS), 128])
        rbr = sb("rbr", [128, E_])
        bqs = sb("bqs", [128, 2])
        ident = sb("ident", [128, 128])
        mats = sb("mats", [128, 2, 128])
        xpos = sb("xpos", [128, 4, 128])
        bfc = sb("bfc", [128, 3, 128], BF16)
        epsc = sb("epsc", [128, 1])

        ps = ctx.enter_context(nc.psum_tensor("ps", [128, 8, 512], F32))
        scores_ps = [ps[:, 0, :], ps[:, 1, :]]
        probsT_ps = [ps[:, 2, :], ps[:, 3, :]]
        out_ps = [ps[:, 4, 0:S], ps[:, 5, 0:S]]
        misc_ps = [ps[:, 6, :], ps[:, 7, :]]

        ld = {name: sem(f"loaded_{name}") for name in t if name != "out"}
        zeroed_bd = [sem(f"zeroed_bd{j}") for j in range(PAIRS)]
        zeroed_vpad = sem("zeroed_vpad")
        consts = sem("consts_ready")
        masks = sem("masks_ready")
        scores = sem("scores")
        negmax = sem("negmax")
        probs_ready = sem("probs_ready")
        probsT = sem("probsT")
        wT = sem("weightsT_ready")
        pv = sem("pv")
        stat_ready = sem("stat_ready")
        vpad_ready = sem("vpad_ready")
        recip_ready = sem("recip_ready")
        rexp_ready = sem("rexp_ready")
        rTs_ready = sem("rTs_ready")
        out_taken = sem("out_taken")
        misc_ready = [sem(f"misc_ready{n}") for n in range(2)]
        z_ready = sem("z_ready")
        routed = sem("routed")
        k4_cos, k4_sin = sem("k4_cos"), sem("k4_sin")
        q4_cos, q4_sin = sem("q4_cos"), sem("q4_sin")
        bd_ready = [[sem(f"bd_ready{j}_{g}") for g in range(GROUPS)] for j in range(PAIRS)]
        kT_ready = [sem("kT0_ready"), sem("kT1_ready")]
        q4_ready = sem("q4T_ready")
        statT_ready = [sem(f"statT{n}_ready") for n in range(3)]
        vals_ready = [sem(f"vals{n}_ready") for n in range(3)]
        mv_ready = sem("variance_ready")
        rstd_ready = sem("rstd_ready")
        x_ready = sem("x_ready")
        xb_ready = sem("xb_ready")
        xTs_ready = sem("xTs_ready")
        lsub_ready = sem("lsub_ready")
        lexp_ready = sem("lexp_ready")
        gated_ready = sem("gated_ready")
        gatedT_ready = sem("gatedT_ready")
        p_ready = sem("p_ready")
        pads = sem("pads_ready")
        taps_done = sem("taps_done")
        products = sem("products")
        pool_taps = sem("pool_taps")
        silu_ready = sem("silu_ready")
        ret_ready = sem("ret_ready")
        cen_ready = sem("cen_ready")
        sq_ready = sem("sq_ready")
        sd_ready = sem("sd_ready")
        rg_ready = sem("rg_ready")
        hid_ps = sem("hidden_in_psum")
        gateA_ready = sem("gateA_ready")
        hid_ready = [sem(f"hidden{n}_ready") for n in range(3)]
        y_ps = sem("ffn_y_in_psum")
        y_free = sem("ffn_y_free")
        out_done = sem("out_done")
        dve_own = sem("dve_own")
        act_own = sem("act_own")
        pool_own = sem("pool_own")

        block = ctx.enter_context(nc.Block())

        def misc(item, n=0):
            at = misc_at[item] + n
            return misc_ps[at % 2], at % 2, at // 2

        def wait_misc(engine, item, n=0):
            _, i, before = misc(item, n)
            engine.wait_ge(misc_ready[i], before + 1)

        def bcast(ap, n):
            return ap.unsqueeze(1).broadcast_to([128, n, ap.shape[-1]])

        def inner(ap, n):
            return ap.unsqueeze(2).broadcast_to([128, ap.shape[-1], n])

        def col(name, n=0):
            return cols[:, COLS[name] + n:COLS[name] + n + 1]

        def row(name):
            return rows[:, ROWS[name], :]

        def pair(tensor, j):
            return tensor[:, 2 * S * j:2 * S * (j + 1)]

        def norm_no(n, j):
            return norm_at[(n, j)]

        norm_at = {}
        for item in order:
            if item[0] == "rstd":
                norm_at[item[1:]] = len(norm_at)

        def xT_no(n, j):
            return [i[1:] for i in order if i[0] == "xT"].index((n, j))

        def split_taps(first, n, c):
            return range(first + n * c // CHUNKS, first + n * (c + 1) // CHUNKS)

        def walk():
            for k in range(WALK_STEPS):
                for v in range(UNITS):
                    yield k, v, schedule.get((k, v), [])

        LAST = UNITS * CORE_STEPS
        bias_of = {0: "bo1", 1: "base_b", 2: "bias2", 3: "out_b"}

        reader, z_seen = [], 0
        for item in order:
            kind, arg = item[0], item[1:]
            if kind == "projK":
                reader.append((kT_ready[arg[0]], arg[1] + 1))
            elif kind == "projQ0":
                reader.append((statT_ready[0], arg[0] + 1))
            elif kind == "projV":
                reader.append((vals_ready[arg[0]], arg[1] + 1))
            elif kind == "projK4":
                reader += [(k4_cos, arg[0] + 1), (k4_sin, arg[0] + 1)]
            elif kind == "projQ1":
                reader.append((statT_ready[1], arg[0] + 1))
            elif kind == "rT":
                reader.append((rTs_ready, seq_no(*arg) + 1))
            elif kind == "y":
                z_seen += 1
                reader.append((z_ready, z_seen))
            elif kind == "xT":
                reader.append((xTs_ready, xT_no(*arg) + 1))
            elif kind == "route":
                reader.append((routed, arg[0] + 1))
            elif kind == "experts":
                z_seen += 2
                reader += [(gatedT_ready, arg[0] + 1), (z_ready, z_seen)]
            elif kind in ("memY", "retY"):
                z_seen += 2
                reader.append((z_ready, z_seen))
            elif kind == "projP":
                reader.append((p_ready, arg[0] + 1))
            elif kind == "projQ4":
                reader += [(q4_cos, arg[0] + 1), (q4_sin, arg[0] + 1)]
            elif kind == "silu":
                reader.append((silu_ready, arg[0] + 1))
            elif kind == "center":
                reader.append((cen_ready, arg[0] + 1))
            elif kind == "spread":
                reader.append((sd_ready, arg[0] + 1))
            elif kind == "ffY":
                z_seen += 2
                reader.append((y_free, arg[0] + 1))
        misc_total = len(reader)
        assert misc_total == n_misc
        for kind in ("apply", "xT"):
            seen = [i[1:] for i in order if i[0] == kind]
            want = [i[1:] for i in order if i[0] == "rstd" and (kind == "apply" or i[1] < 5)]
            assert seen == want, (kind, seen, want)

        ffn_no, ffn_at, ffn_before, last_in, turn = {}, [], [], {}, 0
        for k in range(WALK_STEPS):
            for v in range(UNITS):
                for item in schedule.get((k, v), []):
                    if item[0] != "ff":
                        continue
                    n = ffn_no[item[1:]] = len(ffn_at)
                    ring = (2, 3) if (k, v) < (CORE_STEPS, 5) else (2, 3, 0, 1, 4, 5)
                    bank = ring[turn % len(ring)]
                    turn += 1
                    ffn_at.append(bank)
                    ffn_before.append(last_in.get(bank))
                    last_in[bank] = item[1:]

        def ffn_ps(item):
            return ps[:, ffn_at[ffn_no[item]], :]

        def hid_reader(item):
            j, layer, m = item
            return hid_ready[layer], (KT if layer == 0 else 2) * j + m + 1

        xb_at = {}
        for j in range(PAIRS):
            xb_at[(0, j)] = len(xb_at)
        for item in order:
            if item[0] == "apply" and item[1] in bias_of:
                xb_at[(item[1] + 1, item[2])] = len(xb_at)

        def xb_before(n, j):
            return xb_at[(n, j)] + 1

        def norm_rstd(n, j, pool):
            m = n if n < 5 else 0
            pool.wait_ge(mv_ready, norm_no(n, j) + 1)
            pool.tensor_tensor(rstd[:, m, 2 * j:2 * j + 2], vpe[:, m, 2 * j:2 * j + 2], mhalf[:, :].broadcast_to([128, 2]),
                               ALU.pow).then_inc(pool_own, 1)
            pool.wait_ge(pool_own, norm_no(n, j) + 1)
            pool.tensor_tensor(nmr[:, m, 2 * j:2 * j + 2], nmean[:, m, 2 * j:2 * j + 2], rstd[:, m, 2 * j:2 * j + 2],
                               ALU.mult).then_inc(rstd_ready, 1)

        @block.sync
        def _(sp):
            for name, dst in (("w0", w0[:, :, :]), ("xT0", xT0[:, :]), ("cols", cols[:, :]), ("bfc", bfc[:, :, :]),
                              ("rows", rows[:, :, :]), ("ident", ident[:, :]), ("ctxT", ctxT[:, :]), ("w1", w1[:, :, :]),
                              ("X", X[:, :, :]), ("maskI", maskI[:, :, :]), ("gT", gT[:, :, :]), ("wr", wr[:, :, :]),
                              ("xpos", xpos[:, :, :])):
                sp.dma_start(dst, t[name]).then_inc(ld[name], 16)

            def spread_heads(core, j):
                sp.wait_ge(zeroed_bd[j], 1)
                if core == RET:
                    sp.wait_ge(q4_ready, j + 1)
                    src = q4T
                else:
                    sp.wait_ge(kT_ready[core], j // 2 + 1)
                    src = kT[:, core, :]
                if core > A0:
                    sp.wait_ge(scores, UNITS * (STEP_OF[core - 1, j] + 1))
                for h in range(H):
                    p = slice(DH * h, DH * (h + 1))
                    s_ = (src[p, 2 * S * j:2 * S * (j + 1)]).rearrange("p (b s) -> p b s", b=2)
                    sp.dma_start(bd[p, 2 * j:2 * j + 2, h, :], s_).then_inc(bd_ready[j][h // HG], 16)

            for item in PROLOGUE:
                if item[0] == "bd":
                    spread_heads(*item[1:])
            for name, dst in (("wm", wm[:, :]), ("rbr", rbr[:, :]), ("wf", wf[:, :, :]), ("causalT", causalT[:, :]),
                              ("mats", mats[:, :, :])):
                sp.dma_start(dst, t[name]).then_inc(ld[name], 16)
            for k, v, items in walk():
                for item in items:
                    if item[0] == "bd":
                        spread_heads(*item[1:])
                    if item[:2] == ("apply", 5):
                        j = item[2]
                        sp.wait_ge(x_ready, norm_no(5, j) + 1)
                        sp.dma_start(t["out"][:, 2 * j:2 * j + 2, :], X[:, 2 * j:2 * j + 2, :]).then_inc(out_done, 16)
                if (k, v) == (STEP_OF[A0, 3] + 1, 2):
                    for groups in bd_ready:
                        for n in groups:
                            sp.wait_ge(n, 16 * HG * 2)
                    sp.wait_ge(masks, 1)
                    sp.wait_ge(vals_ready[0], 2)
                    sp.wait_ge(statT_ready[0], 2)
                    sp.dma_start(wh[:, :, :, :], t["wh"]).then_inc(ld["wh"], 16)
                if (k, v) == (8, 2):
                    sp.wait_ge(wT, 16 * GROUPS)
                    sp.wait_ge(scores, 16 * GROUPS)
                    sp.dma_start(wi[:, :, :], t["wi"]).then_inc(ld["wi"], 16)
                    sp.dma_start(wo3[:, :, :], t["wo3"]).then_inc(ld["wo3"], 16)
            sp.wait_ge(out_done, 16 * PAIRS)

        @block.gpsimd
        def _(pool):
            pool.memset(mhalf[:, :], -0.5)
            pool.memset(epsc[:, :], EPS)
            pool.memset(pPad[:, :, :, :], 0.0).then_inc(pads, 1)
            for j in (2, 3):
                pool.memset(bd[:, 2 * j:2 * j + 2, :, :], 0.0).then_inc(zeroed_bd[j], 1)

            def stage_in(core, j, e):
                b, n = 2 * j + e, 2 * STEP_OF[core, j] + e
                if n >= 2:
                    pool.wait_ge(scores, GROUPS * (n - 1))
                pool.wait_ge(statT_ready[core], b // 4 + 1 if core != A1 else j + 1)
                pool.tensor_copy(stat[:, e, :], statT[:, core, S * b:S * (b + 1)]).then_inc(stat_ready, 1)
                if n >= 2:
                    pool.wait_ge(pv, GROUPS * (n - 1))
                else:
                    pool.wait_ge(zeroed_vpad, 1)
                pool.wait_ge(vals_ready[core], b // 4 + 1)
                blocks = vpad[:, e, :, :].rearrange("p h d -> p (h d)")
                diag = bass_diag(blocks)
                pool.tensor_copy(diag, vals[:, core, b, :].rearrange("p (h d) -> p h d", h=H)).then_inc(vpad_ready, 1)

            def bass_diag(flat):
                ap = flat[:, 0:H * DH].rearrange("p (h d) -> p h d", h=H)
                return bass.AP(ap.tensor, ap.offset, [list(ap.ap[0]), [D + DH, H], [1, DH]])

            stage_in(A0, 0, 0)
            for b in range(B):
                if b == 0:
                    pool.wait_ge(ld["X"], 16)
                    pool.wait_ge(ld["rows"], 16)
                if b % 2 == 0:
                    pool.tensor_tensor(XB[:, b:b + 2, :], X[:, b:b + 2, :], bcast(row("bo0"), 2), ALU.add).then_inc(xb_ready, 1)
            for k, v, items in walk():
                nxt = None
                if v == 0 and k < CORE_STEPS:
                    nxt = (*STEPS[k], 1)
                if v == 4 and k + 1 < CORE_STEPS:
                    nxt = (*STEPS[k + 1], 0)
                if nxt:
                    stage_in(*nxt)
                for item in items:
                    if item[0] == "recip":
                        c, b = item[1:]
                        n = seq_no(c, b)
                        pool.wait_ge(recip_ready, n + 1)
                        if n >= 2:
                            core, b_, _, _ = unit(GROUPS * (n - 2))
                            wait_misc(pool, ("rT", core, b_))
                        pool.tensor_copy(rexp[:, b % 2, :, :], inner(recip[:, b % 2, :], DH)).then_inc(rexp_ready, 1)
                    if item[0] == "taps":
                        j, c = item[1:]
                        for i in split_taps(TAPS - POOL_TAPS, POOL_TAPS, c):
                            if i == TAPS - POOL_TAPS:
                                continue
                            n = i - (TAPS - POOL_TAPS) + POOL_TAPS * j
                            pool.wait_ge(products, n - j)
                            pool.wait_ge(pool_taps, n)
                            pool.tensor_tensor(memP[:, j % 2, :, :], memP[:, j % 2, :, :], prod[:, n % PRODUCTS, :, :],
                                               ALU.add).then_inc(pool_taps, 1)
                    if item[0] == "rstd":
                        norm_rstd(item[1], item[2], pool)
                    if item[0] == "apply" and item[1] in bias_of:
                        n, j = item[1:]
                        pool.wait_ge(x_ready, norm_no(n, j) + 1)
                        pool.tensor_tensor(XB[:, 2 * j:2 * j + 2, :], X[:, 2 * j:2 * j + 2, :], bcast(row(bias_of[n]), 2),
                                           ALU.add).then_inc(xb_ready, 1)

        @block.scalar
        def _(act):
            own = [0]

            def link(ins):
                own[0] += 1
                ins.then_inc(act_own, 1)
                act.wait_ge(act_own, own[0])

            def ready(item, n=0):
                bank, i, before = misc(item, n)
                act.wait_ge(misc_ready[i], before + 1)
                return bank

            def exps(u):
                core, b, g, e = unit(u)
                act.wait_ge(negmax, u + 1)
                if u >= 2:
                    act.wait_ge(probsT, u - 1)
                for i in range(HG):
                    last = act.activation(probs[:, u % 2, S * i:S * (i + 1)], scores_ps[u % 2][:, S * i:S * (i + 1)], ACT.Exp,
                                          bias=nmax[:, u % UNITS, i:i + 1],
                                          accum_out=rowsum[:, e, HG * g + i:HG * g + i + 1])
                last.then_inc(probs_ready, 1)

            def run(item):
                kind, arg = item[0], item[1:]
                if kind == "projK":
                    c, h = arg
                    bank = ready(item)
                    act.activation(kT[:, c, 512 * h:512 * (h + 1)], bank, ACT.Identity,
                                   bias=col("bk0" if c == 0 else "bk1")).then_inc(kT_ready[c], 1)
                elif kind == "projQ0":
                    h, = arg
                    bank = ready(item)
                    act.wait_ge(consts, 1)
                    act.activation(statT[:, 0, 512 * h:512 * (h + 1)], bank, ACT.Identity, bias=bqs[:, 0:1],
                                   scale=SCALE).then_inc(statT_ready[0], 1)
                elif kind == "projQ1":
                    j, = arg
                    bank = ready(item)
                    act.activation(pair(statT[:, 1, :], j), bank[:, 0:2 * S], ACT.Identity, bias=bqs[:, 1:2],
                                   scale=SCALE).then_inc(statT_ready[1], 1)
                elif kind == "rT":
                    c, b = arg
                    bank = ready(item)
                    n = seq_no(c, b)
                    if n >= 2:
                        act.wait_ge(out_taken, n - 1)
                    act.copy(rTs[:, b % 2, :], bank[:, 0:S]).then_inc(rTs_ready, 1)
                elif kind == "xT":
                    n, j = arg
                    bank = ready(item)
                    act.copy(xTs[:, n, :] if n < 4 else x5T[:, j, :], bank[:, 0:2 * S]).then_inc(xTs_ready, 1)
                elif kind == "apply":
                    n, j = arg
                    m = n if n < 5 else 0
                    act.wait_ge(rstd_ready, norm_no(n, j) + 1)
                    if n < 5:
                        act.wait_ge(xb_ready, xb_before(n, j))
                    for b in (2 * j, 2 * j + 1):
                        last = act.activation(X[:, b, :], Z[:, b, :], ACT.Identity, bias=nmr[:, m, b:b + 1],
                                              scale=rstd[:, m, b:b + 1])
                    last.then_inc(x_ready, 1)
                elif kind == "gate":
                    j, = arg
                    act.wait_ge(lsub_ready, j + 1)
                    act.activation(lexp[:, :, :], lsub[:, :, :], ACT.Exp).then_inc(lexp_ready, 1)
                elif kind == "experts":
                    j, = arg
                    bank = ready(item)
                    act.copy(gatedT[:, :], bank[:, 0:2 * S]).then_inc(gatedT_ready, 1)
                elif kind == "projP":
                    j, = arg
                    bank = ready(item)
                    act.wait_ge(pads, 1)
                    if j >= 2:
                        act.wait_ge(taps_done, 2 * (TAPS - POOL_TAPS) * (j - 1))
                    for e in range(2):
                        last = act.activation(pPad[:, j % 2, e, TAPS - 1:PADW], bank[:, S * e:S * (e + 1)], ACT.Identity,
                                              bias=col("bias1"), accum_out=psum_all[:, j % 2, e:e + 1])
                    last.then_inc(p_ready, 1)
                elif kind == "taps":
                    j, c = arg
                    for i in split_taps(TAPS - POOL_TAPS, POOL_TAPS, c):
                        n = i - (TAPS - POOL_TAPS) + POOL_TAPS * j
                        src = pPad[:, j % 2, :, TAPS - 1 - i:TAPS - 1 - i + S]
                        if i == TAPS - POOL_TAPS:
                            act.wait_ge(p_ready, j + 1)
                            act.wait_ge(consts, 2)
                            if j >= 2:
                                wait_misc(act, ("memY", j - 2))
                            if j >= 1:
                                act.wait_ge(pool_taps, n)
                            act.activation(memP[:, j % 2, :, :], src, ACT.Copy, scale=mwd[:, i:i + 1]).then_inc(pool_taps, 1)
                        else:
                            if n >= PRODUCTS:
                                act.wait_ge(pool_taps, n - PRODUCTS + 1)
                            act.activation(prod[:, n % PRODUCTS, :, :], src, ACT.Copy, scale=mwd[:, i:i + 1]).then_inc(products, 1)
                elif kind == "silu":
                    j, = arg
                    bank = ready(item)
                    act.activation(pair(silu, j), bank[:, 0:2 * S], ACT.Silu, bias=col("gb")).then_inc(silu_ready, 1)
                elif kind == "center":
                    j, = arg
                    bank = ready(item)
                    if j >= 2:
                        act.wait_ge(rg_ready, j - 1)
                    act.copy(cen[:, j % 2, :], bank[:, 0:2 * S]).then_inc(cen_ready, 1)
                elif kind == "spread":
                    j, = arg
                    bank = ready(item)
                    act.wait_ge(pads, 1)
                    if j >= 1:
                        act.wait_ge(rg_ready, j)
                    act.activation(sd[:, :], bank[:, 0:2 * S], ACT.Sqrt, bias=epsc[:, :]).then_inc(sd_ready, 1)
                elif kind == "ff":
                    j, layer, m = arg
                    act.wait_ge(hid_ps, ffn_no[arg] + 1)
                    if layer == 0:
                        if KT * j + m >= 2:
                            act.wait_ge(hid_ready[0], KT * j + m - 1)
                        else:
                            act.wait_ge(probsT, SOFTMAX_UNITS)
                        act.activation(gateA[:, m % 2, :], ffn_ps(arg)[:, 0:2 * S], ACT.Silu,
                                       scale=col("s1", m)).then_inc(gateA_ready, 1)
                    else:
                        if j >= 2 and m == 0:
                            if layer == 1:
                                act.wait_ge(hid_ps, ffn_no[(j - 2, 2, 1)] + 1)
                            else:
                                wait_misc(act, ("ffY", j - 2))
                        if j < 2:
                            act.wait_ge(scores, UNITS * (STEP_OF[RET, layer - 1] + 1))
                        for half in range(2):
                            last = act.activation(hid[layer][:, j % 2, 2 * m + half, :],
                                                  ffn_ps(arg)[:, 2 * S * half:2 * S * (half + 1)], ACT.Gelu,
                                                  scale=col("sh1" if layer == 1 else "sh2", 2 * m + half))
                        last.then_inc(hid_ready[layer], 1)

            act.memzero(vpad[:, :, :, :]).then_inc(zeroed_vpad, 1)
            act.wait_ge(ld["cols"], 16)
            for item in PROLOGUE:
                run(item)
            exps(0)
            for k, v, items in walk():
                u = UNITS * k + v
                if u + 1 < SOFTMAX_UNITS:
                    exps(u + 1)
                for item in items:
                    run(item)

        @block.vector
        def _(dve):
            own = [0]
            z_count = [0]
            tap_count = [0]

            def link(ins):
                own[0] += 1
                ins.then_inc(dve_own, 1)
                dve.wait_ge(dve_own, own[0])

            def ready(item, n=0):
                bank, i, before = misc(item, n)
                dve.wait_ge(misc_ready[i], before + 1)
                return bank

            def row_max(u):
                dve.wait_ge(scores, u + 1)
                dve.tensor_reduce(nmax[:, u % UNITS, :], scores_ps[u % 2].rearrange("p (h k) -> p h k", h=HG), AX.X,
                                  ALU.max, negate=True).then_inc(negmax, 1)

            def take_weights(u):
                core, b, _, _ = unit(u)
                dve.wait_ge(probsT, u + 1)
                if u >= 3:
                    dve.wait_ge(pv, u - 2)
                src = probsT_ps[u % 2].rearrange("p (h q) -> p h q", h=HG)
                if core == A0:
                    dve.tensor_copy(weightsT[:, u % 3, :, :], src).then_inc(wT, 1)
                else:
                    if u == UNITS * STEP_OF[A1, 0]:
                        dve.wait_ge(ld["gT"], 16)
                    dve.tensor_tensor(weightsT[:, u % 3, :, :], src, bcast(gT[:, b, :], HG), ALU.mult).then_inc(wT, 1)

            def decay(u):
                g = u % GROUPS
                dve.wait_ge(scores, u + 1)
                if u == 16 * GROUPS:
                    dve.wait_ge(ld["causalT"], 16)
                dve.wait_ge(pv, u - 2)
                dve.tensor_tensor(weightsT[:, u % 3, :, :], scores_ps[u % 2].rearrange("p (h q) -> p h q", h=HG),
                                  bcast(causalT[:, :], HG), ALU.mult).then_inc(wT, 1)

            def stats(n, sequences, last_op):
                m = n if n < 5 else 0
                z_count[0] += len(sequences)
                last_op.then_inc(z_ready, len(sequences))
                dve.wait_ge(z_ready, z_count[0])
                for b in sequences:
                    last = dve.bn_stats(st6[:, b % 2, :], Z[:, b, :])
                link(last)
                for b in sequences:
                    last = dve.bn_aggr(mv[:, m, b, :], st6[:, b % 2, :])
                link(last)

            def add_eps(n, j):
                m = n if n < 5 else 0
                dve.tensor_scalar(vpe[:, m, 2 * j:2 * j + 2], mv[:, m, 2 * j:2 * j + 2, 1], EPS, None, ALU.add)
                dve.tensor_scalar(nmean[:, m, 2 * j:2 * j + 2], mv[:, m, 2 * j:2 * j + 2, 0], -1.0, None, ALU.mult).then_inc(mv_ready, 1)

            def add_pair(n, j, bank):
                dve.wait_ge(xb_ready, xb_before(n, j))
                stats(n, (2 * j, 2 * j + 1), dve.tensor_tensor(
                    Z[:, 2 * j:2 * j + 2, :], bank[:, 0:2 * D].rearrange("p (e d) -> p e d", e=2),
                    XB[:, 2 * j:2 * j + 2, :], ALU.add))

            def run(item):
                kind, arg = item[0], item[1:]
                if kind == "projV":
                    c, h = arg
                    bank = ready(item)
                    src = bank.rearrange("p (b d) -> p b d", b=4)
                    dst = vals[:, c, 4 * h:4 * h + 4, :]
                    if c == RET:
                        ins = dve.tensor_copy(dst, src)
                    else:
                        dve.wait_ge(ld["rows"], 16)
                        ins = dve.tensor_tensor(dst, src, bcast(row("bv0" if c == 0 else "bv1"), 4), ALU.add)
                    ins.then_inc(vals_ready[c], 1)
                elif kind == "projK4":
                    h, = arg
                    dst = statT[:, 2, 512 * h:512 * (h + 1)].rearrange("p (b s) -> p b s", b=4)
                    dve.wait_ge(ld["xpos"], 16)
                    bank = ready(item)
                    dve.tensor_tensor(dst, bank.rearrange("p (b s) -> p b s", b=4), bcast(xpos[:, 2, :], 4), ALU.mult).then_inc(k4_cos, 1)
                    bank = ready(item, 1)
                    if h:
                        dve.wait_ge(statT_ready[2], h)
                    for i, tmp in enumerate((qa, qb)):
                        last = dve.tensor_tensor(tmp[:, :, :], bank[:, 2 * S * i:2 * S * (i + 1)].rearrange("p (b s) -> p b s", b=2),
                                                 bcast(xpos[:, 3, :], 2), ALU.mult)
                    last.then_inc(k4_sin, 1)
                    dve.wait_ge(k4_sin, h + 1)
                    for i, tmp in enumerate((qa, qb)):
                        last = dve.tensor_tensor(dst[:, 2 * i:2 * i + 2, :], dst[:, 2 * i:2 * i + 2, :], tmp[:, :, :], ALU.add)
                    last.then_inc(statT_ready[2], 1)
                elif kind == "recip":
                    c, b = arg
                    dve.wait_ge(probs_ready, GROUPS * (seq_no(c, b) + 1))
                    if seq_no(c, b) >= 2:
                        dve.wait_ge(rexp_ready, seq_no(c, b) - 1)
                    dve.reciprocal(recip[:, b % 2, :], rowsum[:, b % 2, :]).then_inc(recip_ready, 1)
                elif kind == "outT":
                    c, b = arg
                    n = seq_no(c, b)
                    dve.wait_ge(rTs_ready, n + 1)
                    dve.wait_ge(pv, GROUPS * (n + 1))
                    if n >= 2:
                        core, b_, _, _ = unit(GROUPS * (n - 2))
                        wait_misc(dve, ("y", core, b_))
                    dve.tensor_tensor(outT[:, b % 2, :], out_ps[b % 2], rTs[:, b % 2, :], ALU.mult).then_inc(out_taken, 1)
                elif kind == "y":
                    c, b = arg
                    bank = ready(item)
                    dve.wait_ge(xb_ready, xb_before(c, b // 2))
                    ins = dve.tensor_tensor(Z[:, b, :], bank[:, 0:D], XB[:, b, :], ALU.add)
                    stats(c, (b,), ins)
                elif kind == "rstd":
                    add_eps(*arg)
                elif kind == "route":
                    j, = arg
                    bank = ready(item)
                    dve.wait_ge(ld["rbr"], 16)
                    both = bank[:, 0:2 * (128 + E_)].rearrange("p (e n) -> p e n", e=2)
                    dve.tensor_tensor(lg[:, :, :], both[:, :, 128:], bcast(rbr[:, :], 2), ALU.add)
                    dve.tensor_copy(axs[:, :, :, :].rearrange("p a b c -> p a (b c)"), both[:, :, 0:128]).then_inc(routed, 1)
                    dve.wait_ge(routed, j + 1)
                    dve.max(top[:, 0, :], lg[:, 0, :])
                    link(dve.max(top[:, 1, :], lg[:, 1, :]))
                    dve.tensor_tensor(lsub[:, :, :], lg[:, :, :], inner(top[:, :, 0], E_), ALU.subtract).then_inc(lsub_ready, 1)
                    link(dve.tensor_tensor(keep[:, :, :], lg[:, :, :], inner(top[:, :, 1], E_), ALU.is_ge))
                elif kind == "gate":
                    j, = arg
                    dve.wait_ge(lexp_ready, j + 1)
                    link(dve.tensor_tensor(kept[:, :, :], keep[:, :, :], lexp[:, :, :], ALU.mult))
                    link(dve.tensor_reduce(esum[:, :], kept[:, :, :], AX.X, ALU.add))
                    link(dve.reciprocal(erec[:, :], esum[:, :]))
                    for e in range(2):
                        last = dve.tensor_scalar(wexp[:, e, :], kept[:, e, :], erec[:, e:e + 1], 2.0, ALU.mult, ALU.mult)
                    link(last)
                    for e in range(2):
                        last = dve.tensor_tensor(gated[:, e, :, :], axs[:, e, :, :], inner(wexp[:, e, :], R_), ALU.mult)
                    last.then_inc(gated_ready, 1)
                elif kind == "experts":
                    j, = arg
                    bank = ready(item, 1)
                    add_pair(2, j, bank)
                elif kind == "taps":
                    j, c = arg
                    if c == 0:
                        dve.wait_ge(p_ready, j + 1)
                        if j == 0:
                            dve.wait_ge(consts, 2)
                        if j >= 2:
                            wait_misc(dve, ("memY", j - 2))
                        link(dve.tensor_scalar(ptot[:, j % 2, :], psum_all[:, j % 2, :], col("mw"), None, ALU.mult))
                    for i in split_taps(0, TAPS - POOL_TAPS, c):
                        for e in range(2):
                            acc, src = mem[:, j % 2, e, :], pPad[:, j % 2, e, TAPS - 1 - i:TAPS - 1 - i + S]
                            if i == 0:
                                last = dve.tensor_scalar(acc, src, mwd[:, 0:1], ptot[:, j % 2, e:e + 1], ALU.mult, ALU.add)
                            else:
                                dve.wait_ge(taps_done, tap_count[0] - 1)
                                last = dve.scalar_tensor_tensor(acc, src, mwd[:, i:i + 1], acc, ALU.mult, ALU.add)
                            last.then_inc(taps_done, 1)
                            tap_count[0] += 1
                    if c == CHUNKS - 1:
                        assert tap_count[0] == 2 * (TAPS - POOL_TAPS) * (j + 1)
                elif kind == "memY":
                    j, = arg
                    bank = ready(item)
                    add_pair(3, j, bank)
                elif kind == "projQ4":
                    j, = arg
                    bank = ready(item)
                    if j:
                        dve.wait_ge(q4_ready, j)
                    else:
                        dve.wait_ge(statT_ready[2], 2)
                    dve.tensor_tensor(qa[:, :, :], bank[:, 0:2 * S].rearrange("p (e s) -> p e s", e=2), bcast(xpos[:, 0, :], 2),
                                      ALU.mult).then_inc(q4_cos, 1)
                    bank = ready(item, 1)
                    dve.tensor_tensor(qb[:, :, :], bank[:, 0:2 * S].rearrange("p (e s) -> p e s", e=2),
                                      bcast(xpos[:, 1, :], 2), ALU.mult).then_inc(q4_sin, 1)
                    dve.wait_ge(q4_sin, j + 1)
                    dve.tensor_tensor(pair(q4T, j).rearrange("p (e s) -> p e s", e=2), qa[:, :, :], qb[:, :, :],
                                      ALU.add).then_inc(q4_ready, 1)
                elif kind == "grab":
                    b, = arg
                    n = 2 * B + b
                    dve.wait_ge(pv, GROUPS * (n + 1))
                    if b >= 4:
                        wait_misc(dve, ("center", b // 2 - 2))
                    dve.tensor_copy(ret[:, (b // 2) % 2, S * (b % 2):S * (b % 2 + 1)], out_ps[b % 2]).then_inc(out_taken, 1)
                elif kind == "center":
                    j, = arg
                    dve.wait_ge(cen_ready, j + 1)
                    if j >= 1:
                        wait_misc(dve, ("spread", j - 1))
                    dve.tensor_tensor(sq[:, :], cen[:, j % 2, :], cen[:, j % 2, :], ALU.mult).then_inc(sq_ready, 1)
                elif kind == "spread":
                    j, = arg
                    dve.wait_ge(sd_ready, j + 1)
                    link(dve.reciprocal(rsd[:, :], sd[:, :]))
                    link(dve.tensor_tensor(rg[:, :], cen[:, j % 2, :], rsd[:, :], ALU.mult))
                    dve.wait_ge(silu_ready, j + 1)
                    if j >= 1:
                        wait_misc(dve, ("retY", j - 1))
                    dve.tensor_tensor(rg2[:, :], rg[:, :], pair(silu, j), ALU.mult).then_inc(rg_ready, 1)
                elif kind == "ff" and arg[1] == 0:
                    j, _, m = arg
                    dve.wait_ge(hid_ps, ffn_no[arg] + 1)
                    dve.wait_ge(gateA_ready, KT * j + m + 1)
                    if m == 0 and j >= 2:
                        dve.wait_ge(hid_ps, ffn_no[(j - 2, 1, 1)] + 1)
                    elif m == 0 and j == 0:
                        dve.wait_ge(scores, UNITS * (STEP_OF[RET, 0] + 1))
                    dve.scalar_tensor_tensor(hid[0][:, j % 2, m, :], ffn_ps(arg)[:, 2 * S:4 * S], col("s2", m),
                                             gateA[:, m % 2, :], ALU.mult, ALU.mult).then_inc(hid_ready[0], 1)
                elif kind == "ffY":
                    j, = arg
                    bank = ready(item)
                    dve.tensor_tensor(ysc[:, :, :], bank[:, 0:2 * D].rearrange("p (e d) -> p e d", e=2),
                                      bcast(row("s3"), 2), ALU.mult).then_inc(y_free, 1)
                    dve.wait_ge(y_free, j + 1)
                    dve.wait_ge(x_ready, norm_no(4, j) + 1)
                    stats(5, (2 * j, 2 * j + 1), dve.tensor_tensor(Z[:, 2 * j:2 * j + 2, :], ysc[:, :, :],
                                                                   X[:, 2 * j:2 * j + 2, :], ALU.add))
                elif kind == "retY":
                    j, = arg
                    bank = ready(item)
                    add_pair(4, j, bank)

            for j in (0, 1):
                dve.memset(bd[:, 2 * j:2 * j + 2, :, :], 0.0).then_inc(zeroed_bd[j], 1)
            dve.wait_ge(ld["cols"], 16)
            dve.tensor_scalar(bqs[:, 0:1], col("bq0"), SCALE, None, ALU.mult)
            dve.tensor_scalar(bqs[:, 1:2], col("bq1"), SCALE, None, ALU.mult).then_inc(consts, 1)
            dve.tensor_scalar(mwd[:, :], cols[:, COLS["mw"] + 1:COLS["mw"] + 1 + TAPS], col("mw"), None,
                              ALU.subtract).then_inc(consts, 1)
            for item in PROLOGUE:
                run(item)
            row_max(0)
            for k, v, items in walk():
                u = UNITS * k + v
                if k == 0 and v == 1:
                    dve.wait_ge(ld["maskI"], 16)
                    dve.tensor_scalar(maskHi[:, :, :], maskI[:, :, :], -1.0, MASK_HI, ALU.add, ALU.mult)
                    dve.tensor_scalar(maskLo[:, :, :], maskI[:, :, :], -1.0, MASK_LO, ALU.add, ALU.mult).then_inc(masks, 1)
                if u + 1 < SOFTMAX_UNITS:
                    row_max(u + 1)
                elif u + 1 < LAST:
                    if u + 1 == SOFTMAX_UNITS:
                        take_weights(u)
                    decay(u + 1)
                if u < SOFTMAX_UNITS - 1:
                    take_weights(u)
                for item in items:
                    run(item)

        @block.tensor
        def _(pe):
            def use(item, n=0):
                bank, i, before = misc(item, n)
                if before:
                    pe.wait_ge(*reader[misc_at[item] + n - 2])
                return bank, misc_ready[i]

            def unit_scores(u):
                core, b, g, e = unit(u)
                n = u // GROUPS
                if u >= 2:
                    if u - 2 < SOFTMAX_UNITS:
                        pe.wait_ge(probs_ready, u - 1)
                    else:
                        pe.wait_ge(wT, u - 1)
                if g == 0:
                    pe.wait_ge(stat_ready, n + 1)
                if e == 0:
                    pe.wait_ge(bd_ready[b // 2][g], 16 * HG * (core + 1))
                out = scores_ps[u % 2]
                if core == A0:
                    if u == 0:
                        pe.wait_ge(ld["bfc"], 16)
                    pe.matmul(out, bfc[:, 0, :], bcast(bfc[:, 1, :], HG), start=True, stop=False)
                elif core == A1:
                    if u == UNITS * STEP_OF[A1, 0]:
                        pe.wait_ge(masks, 1)
                    pe.matmul(out, bfc[:, 2, :], bcast(maskHi[:, b, :], HG), start=True, stop=False)
                    pe.matmul(out, bfc[:, 2, :], bcast(maskLo[:, b, :], HG), start=False, stop=False)
                pe.matmul(out, stat[:, e, :], bd[:, b, HG * g:HG * (g + 1), :].rearrange("p h s -> p (h s)"),
                          start=(core == RET), stop=True).then_inc(scores, 1)

            def unit_transposes(u):
                pe.wait_ge(probs_ready, u + 1)
                if u >= 2:
                    pe.wait_ge(wT, u - 1)
                for i in range(HG):
                    last = pe.transpose(probsT_ps[u % 2][:, S * i:S * (i + 1)], probs[:, u % 2, S * i:S * (i + 1)], ident[:, :])
                last.then_inc(probsT, 1)

            def unit_pv(u):
                n, g, e = u // GROUPS, u % GROUPS, (u // GROUPS) % 2
                pe.wait_ge(wT, u + 1)
                if g == 0:
                    pe.wait_ge(vpad_ready, n + 1)
                    if n >= 2:
                        pe.wait_ge(out_taken, n - 1)
                for i in range(HG):
                    h = HG * g + i
                    last = pe.matmul(out_ps[e], vpad[:, e, h, :], weightsT[:, u % 3, i, :], start=(h == 0), stop=(h == H - 1))
                last.then_inc(pv, 1)

            def run(item):
                kind, arg = item[0], item[1:]
                if kind in ("projK", "projQ0", "projV"):
                    c, h = arg if kind != "projQ0" else (0, *arg)
                    src = xT0 if c == 0 else ctxT
                    pe.wait_ge(ld["xT0" if c == 0 else "ctxT"], 16)
                    pe.wait_ge(ld[("w0", "w1", "wr")[c]], 16)
                    w = (w0, w1, wr)[c]
                    bank, rd = use(item)
                    if kind == "projV":
                        for b in range(4 * h, 4 * h + 4):
                            last = pe.matmul(bank[:, D * (b % 4):D * (b % 4 + 1)], src[:, S * b:S * (b + 1)],
                                             w[:, 2 if c != RET else 4, :], start=True, stop=True)
                    else:
                        last = pe.matmul(bank, w[:, 1 if kind == "projQ0" else 0, :], src[:, 512 * h:512 * (h + 1)],
                                         start=True, stop=True)
                    last.then_inc(rd, 1)
                elif kind == "projK4":
                    h, = arg
                    for n in range(2):
                        bank, rd = use(item, n)
                        pe.wait_ge(ld["wr"], 16)
                        pe.matmul(bank, wr[:, 2 + n, :], ctxT[:, 512 * h:512 * (h + 1)], start=True, stop=True).then_inc(rd, 1)
                elif kind == "projQ1":
                    j, = arg
                    bank, rd = use(item)
                    pe.wait_ge(xTs_ready, xT_no(0, j) + 1)
                    pe.matmul(bank[:, 0:2 * S], w1[:, 1, :], xTs[:, 0, :], start=True, stop=True).then_inc(rd, 1)
                elif kind == "rT":
                    c, b = arg
                    bank, rd = use(item)
                    pe.wait_ge(rexp_ready, seq_no(c, b) + 1)
                    pe.transpose(bank[:, 0:S], rexp[:, b % 2, :, :].rearrange("p h d -> p (h d)"), ident[:, :]).then_inc(rd, 1)
                elif kind == "y":
                    c, b = arg
                    bank, rd = use(item)
                    pe.wait_ge(out_taken, seq_no(c, b) + 1)
                    pe.matmul(bank[:, 0:D], outT[:, b % 2, :], (w0, w1)[c][:, 3, :], start=True, stop=True).then_inc(rd, 1)
                elif kind == "xT":
                    n, j = arg
                    bank, rd = use(item)
                    pe.wait_ge(x_ready, norm_no(n, j) + 1)
                    for e in range(2):
                        last = pe.transpose(bank[:, S * e:S * (e + 1)], X[:, 2 * j + e, :], ident[:, :])
                    last.then_inc(rd, 1)
                elif kind == "route":
                    j, = arg
                    bank, rd = use(item)
                    pe.wait_ge(ld["wm"], 16)
                    pe.wait_ge(xTs_ready, xT_no(1, j) + 1)
                    N = 128 + E_
                    for e in range(2):
                        last = pe.matmul(bank[:, N * e:N * (e + 1)], xTs[:, 1, S * e:S * (e + 1)], wm[:, 256:256 + N],
                                         start=True, stop=True)
                    last.then_inc(rd, 1)
                elif kind == "experts":
                    j, = arg
                    bank, rd = use(item)
                    pe.wait_ge(gated_ready, j + 1)
                    for e in range(2):
                        last = pe.transpose(bank[:, S * e:S * (e + 1)], gated[:, e, :, :].rearrange("p a b -> p (a b)"), ident[:, :])
                    last.then_inc(rd, 1)
                    bank, rd = use(item, 1)
                    pe.wait_ge(gatedT_ready, j + 1)
                    for e in range(2):
                        pe.matmul(bank[:, D * e:D * (e + 1)], xTs[:, 1, S * e:S * (e + 1)], wm[:, 0:128], start=True, stop=False)
                        last = pe.matmul(bank[:, D * e:D * (e + 1)], gatedT[:, S * e:S * (e + 1)], wm[:, 128:256],
                                         start=False, stop=True)
                    last.then_inc(rd, 1)
                elif kind == "projP":
                    j, = arg
                    bank, rd = use(item)
                    pe.wait_ge(ld["wf"], 16)
                    pe.wait_ge(xTs_ready, xT_no(2, j) + 1)
                    pe.matmul(bank[:, 0:2 * S], wf[:, 0, :], xTs[:, 2, :], start=True, stop=True).then_inc(rd, 1)
                elif kind == "memY":
                    j, = arg
                    bank, rd = use(item)
                    pe.wait_ge(taps_done, 2 * (TAPS - POOL_TAPS) * (j + 1))
                    pe.wait_ge(pool_taps, POOL_TAPS * (j + 1))
                    for e in range(2):
                        pe.matmul(bank[:, D * e:D * (e + 1)], mem[:, j % 2, e, :], wf[:, 1, :], start=True, stop=False)
                        last = pe.matmul(bank[:, D * e:D * (e + 1)], memP[:, j % 2, e, :], wf[:, 1, :], start=False, stop=True)
                    last.then_inc(rd, 1)
                elif kind == "projQ4":
                    j, = arg
                    for n in range(2):
                        bank, rd = use(item, n)
                        pe.wait_ge(xTs_ready, xT_no(3, j) + 1)
                        pe.matmul(bank[:, 0:2 * S], wr[:, n, :], xTs[:, 3, :], start=True, stop=True).then_inc(rd, 1)
                elif kind == "silu":
                    j, = arg
                    bank, rd = use(item)
                    pe.matmul(bank[:, 0:2 * S], wr[:, 5, :], xTs[:, 3, :], start=True, stop=True).then_inc(rd, 1)
                elif kind == "center":
                    j, = arg
                    bank, rd = use(item)
                    pe.wait_ge(ld["mats"], 16)
                    pe.wait_ge(out_taken, 2 * B + 2 * j + 2)
                    pe.matmul(bank[:, 0:2 * S], mats[:, 1, :], ret[:, j % 2, :], start=True, stop=True).then_inc(rd, 1)
                elif kind == "spread":
                    j, = arg
                    bank, rd = use(item)
                    pe.wait_ge(sq_ready, j + 1)
                    pe.matmul(bank[:, 0:2 * S], mats[:, 0, :], sq[:, :], start=True, stop=True).then_inc(rd, 1)
                elif kind == "retY":
                    j, = arg
                    bank, rd = use(item)
                    pe.wait_ge(rg_ready, j + 1)
                    for e in range(2):
                        last = pe.matmul(bank[:, D * e:D * (e + 1)], rg2[:, S * e:S * (e + 1)], wr[:, 6, :], start=True, stop=True)
                    last.then_inc(rd, 1)

                elif kind == "ff":
                    j, layer, m = arg
                    n = ffn_no[arg]
                    if n == 0:
                        pe.wait_ge(ld["wi"], 16)
                    if ffn_before[n]:
                        pe.wait_ge(*hid_reader(ffn_before[n]))
                    elif ffn_at[n] in (2, 3):
                        pe.wait_ge(wT, SOFTMAX_UNITS)
                    elif ffn_at[n] in (0, 1):
                        pe.wait_ge(wT, LAST)
                    else:
                        pe.wait_ge(out_taken, 3 * B)
                    bank = ffn_ps(arg)
                    if layer == 0:
                        pe.wait_ge(xTs_ready, xT_no(4, j) + 1)
                        for i in range(2):
                            last = pe.matmul(bank[:, 2 * S * i:2 * S * (i + 1)], wi[:, i, 128 * m:128 * (m + 1)],
                                             x5T[:, j, :], start=True, stop=True)
                    else:
                        if layer == 1 and j == 0:
                            pe.wait_ge(ld["wh"], 16)
                        pe.wait_ge(hid_ready[layer - 1], KT * (j + 1) if layer == 1 else 2 * (j + 1))
                        for half in range(2):
                            o = 128 * (2 * m + half)
                            for c in range(KT):
                                last = pe.matmul(bank[:, 2 * S * half:2 * S * (half + 1)], wh[:, layer - 1, c, o:o + 128],
                                                 hid[layer - 1][:, j % 2, c, :], start=(c == 0), stop=(c == KT - 1))
                    last.then_inc(hid_ps, 1)
                elif kind == "ffY":
                    j, = arg
                    bank, rd = use(item)
                    if j == 0:
                        pe.wait_ge(ld["wo3"], 16)
                    pe.wait_ge(hid_ready[2], 2 * (j + 1))
                    for e in range(2):
                        for c in range(KT):
                            last = pe.matmul(bank[:, D * e:D * (e + 1)], hid[2][:, j % 2, c, S * e:S * (e + 1)],
                                             wo3[:, c, :], start=(c == 0), stop=(c == KT - 1))
                    last.then_inc(rd, 1)

            for item in PROLOGUE:
                run(item)
            pe.wait_ge(ld["ident"], 16)
            unit_scores(0)
            for k, v, items in walk():
                u = UNITS * k + v
                if u + 1 < LAST:
                    unit_scores(u + 1)
                if u < SOFTMAX_UNITS:
                    unit_transposes(u)
                for item in items:
                    run(item)
                if 1 <= u <= LAST:
                    unit_pv(u - 1)


_IN = {"float32": F32, "bfloat16": BF16, "int32": I32}


def shape_constants():
    import numpy as np

    f = np.float32
    eye = np.eye(128, dtype=f)
    group = np.kron(np.eye(H, dtype=f), np.full((DH, DH), 1 / DH, f))
    mats = np.stack([group, eye - group], 1)
    pos = np.arange(S)
    bfc = np.stack([-1e10 * eye, (pos[None, :] > pos[:, None]).astype(f), MASK_DIAG * eye], 1).astype(mybir.dt.np(BF16))
    half = DH // 2
    base = ((np.arange(0, DH, 2, dtype=f) + f(0.4 * DH)) / f(1.4 * DH)).astype(f)
    power = (np.arange(-(S // 2), -(S // 2) + S, dtype=f) / f(512.0))[:, None]
    scale = (base[None, :] ** power).astype(f)
    inv_freq = (f(1.0) / f(10000.0) ** (np.arange(half, dtype=f) / f(half))).astype(f)
    ang = (np.arange(S, dtype=f)[:, None] * inv_freq[None, :]).astype(f)
    sin, cos = np.sin(ang), np.cos(ang)
    sign = np.tile(np.array([-1, 1], f), half)
    tables = []
    for s_ in (scale, f(1.0) / scale):
        tables.append(np.repeat(cos * s_, 2, axis=-1))
        tables.append(np.repeat(sin * s_, 2, axis=-1) * sign)
    xpos = np.stack([np.tile(a.T, (H, 1)) for a in tables], 1)
    gammas = (1.0 - np.exp(np.linspace(np.log(1 / 32), np.log(1 / 512), H, dtype=f))).astype(f)
    growth = np.repeat(gammas.astype(np.float64), DH)[:, None] ** (pos - S // 2)[None, :]
    xpos = (xpos * np.stack([growth, growth, 1 / growth, 1 / growth], 1)).astype(f)
    causal = (pos[:, None] <= pos[None, :]).astype(f)
    return dict(ident=eye, mats=mats, bfc=bfc, xpos=xpos, causalT=causal)


def lay_out(i):
    import numpy as np

    def blocks(w):
        return w.reshape(-1, 128, w.shape[-1]).transpose(1, 0, 2)

    def heads(w):
        return w.transpose(1, 0, 2).reshape(D, D)

    def swapped(w):
        return w.reshape(D, -1, 2)[:, :, ::-1].reshape(D, D)

    features = lambda x: x.transpose(2, 0, 1).reshape(D, B * S)
    column = lambda v: v.reshape(-1, 128).T
    wq, wk, wv = (heads(i[f"L1_xattn_W_{n}"]) for n in "QKV")
    a = {
        "X": i["x"].transpose(1, 0, 2),
        "xT0": features(i["x"]),
        "ctxT": features(i["ctx_1024"]),
        "gT": i["fside_BxSxS2_0"].transpose(2, 0, 1),
        "maskI": i["mask_BxSxS2_ik1"].transpose(1, 0, 2),
        "w0": np.stack([i[f"L0_attn_W{n}"].T for n in "kqvo"], 1),
        "w1": np.stack([i[f"L0_xattn_w{n}_k"] for n in "kqvo"], 1),
        "wr": np.stack([wq, swapped(wq), wk, swapped(wk), wv, i["L1_xattn_g_w"].T, i["L1_xattn_out_w"].T], 1),
        "wm": np.concatenate([i["L0_ffn_base_w"].T, i["L0_ffn_lora_B"].reshape(E_ * R_, D),
                              i["L0_ffn_lora_A"].transpose(1, 0, 2).reshape(D, E_ * R_), i["L0_ffn_router_w"].T], 1),
        "wf": np.stack([i["L1_attn_W1"], i["L1_attn_W2"]], 1),
        "wi": np.stack([i["L1_ffn_w1_w"].T, i["L1_ffn_w2_w"].T], 1),
        "wh": np.stack([blocks(i["L1_ffn_h1_w"].T), blocks(i["L1_ffn_h2_w"].T)], 1),
        "wo3": blocks(i["L1_ffn_w3_w"].T),
        "cols": np.concatenate([column(i[n]) for n in (
            "L0_attn_bq", "L0_attn_bk", "L0_xattn_wq_b", "L0_xattn_wk_b", "L1_attn_bias1", "L1_xattn_g_b", "L1_ffn_w1_s",
            "L1_ffn_w2_s", "L1_ffn_h1_s", "L1_ffn_h2_s")] + [i["L1_attn_memory_weights"].T], 1),
        "rows": np.broadcast_to(np.stack([i[n] for n in (
            "L0_attn_bv", "L0_attn_bo", "L0_xattn_wv_b", "L0_xattn_wo_b", "L0_ffn_base_b", "L1_attn_bias2", "L1_xattn_out_b",
            "L1_ffn_w3_s")]), (128, len(ROWS), 128)),
        "rbr": np.broadcast_to(i["L0_ffn_router_b"], (128, E_)),
    }
    return {name: np.ascontiguousarray(v) for name, v in a.items()}


def kernel(**inputs):
    import numpy as np
    import concourse.bacc as bacc
    from concourse.bass_utils import run_bass_kernel_spmd

    nc = bacc.Bacc("TRN2", target_bir_lowering=False, num_devices=1)
    arrays = lay_out({name: np.asarray(a) for name, a in inputs.items()}) | shape_constants()
    t = {name: nc.dram_tensor(f"in_{name}", a.shape, _IN[a.dtype.name], kind="ExternalInput").ap()
         for name, a in arrays.items()}
    t["out"] = nc.dram_tensor("out", (128, B, D), F32, kind="ExternalOutput").ap()
    build(nc, t)
    r = run_bass_kernel_spmd(nc, [{f"in_{name}": a for name, a in arrays.items()}], core_ids=[0])
    return np.ascontiguousarray(r.results[0]["out"].transpose(1, 0, 2))
```

```python
from contextlib import ExitStack
import math

import concourse.bass as bass
from concourse import mybir
from concourse.alu_op_type import AluOpType as ALU

F32 = mybir.dt.float32
BF16 = mybir.dt.bfloat16
I32 = mybir.dt.int32
ACT = mybir.ActivationFunctionType
AX = mybir.AxisListType

B, S, D = 8, 128, 128
H, DH = 16, 8
PAIRS = B // 2
HG = 4
COLG = 32
GROUPS = H // HG
UNITS = 2 * GROUPS
E_, R_ = 8, 16
TAPS = 40
PE_TAPS = 17
POOL_TAPS = 10
DVE_TAPS = TAPS - PE_TAPS - POOL_TAPS
PRODUCTS = 3
CHUNKS = 1
HID = 512
KT = HID // 128
EPS = 1e-5
SCALE = 1.0 / math.sqrt(DH)
MASK_DIAG, MASK_HI, MASK_LO = 64000.0, 15616.0, 9.0
A0, A1, RET = 0, 1, 2
CORE_STEPS = 3 * PAIRS

COLS = dict(bq0=0, bk0=1, bq1=2, bk1=3, bias1=4, gb=5, s1=6, s2=10, sh1=14, sh2=18, mw=22)
NCOLS = 22 + TAPS + 1
ROWS = dict(bv0=0, bo0=1, bv1=2, bo1=3, base_b=4, bias2=5, out_b=6, s3=7)


STEPS = [(A0, 0), (A0, 1), (A0, 2), (A1, 0), (A0, 3), (A1, 1), (A1, 2), (A1, 3), (RET, 0), (RET, 1), (RET, 2), (RET, 3)]
STEP_OF = {cp: k for k, cp in enumerate(STEPS)}
SOFTMAX_UNITS = 2 * PAIRS * UNITS
assert all((core == RET) == (k >= 2 * PAIRS) for k, (core, j) in enumerate(STEPS))


def unit(u):
    core, j = STEPS[u // UNITS]
    e, g = (u // GROUPS) % 2, u % GROUPS
    return core, 2 * j + e, g, e


def head_of(g, i):
    return HG * i + g


def seq_no(core, b):
    return 2 * STEP_OF[core, b // 2] + b % 2


PLACE = {
    "recip": 2, "rT": 4, "outT": 5, "y": 7,
    "rstd0": 11, "apply0": 13, "xT0": 15, "projQ1": 18, "bd1": 10,
    "rstd1": 11, "apply1": 12, "xT1": 13, "route": 14, "gate": 15, "gatedT": 17, "experts": 18,
    "rstd2": 18, "apply2": 19, "xT2": 20, "projP": 21, "taps": 22, "memY": 24,
    "rstd3": 24, "apply3": 26, "xT3": 27, "projQ4": 29, "bd2": 31, "silu": 29,
    "grab": 4, "center": 10, "spread": 10, "retY": 12, "rstd4": 13, "apply4": 14, "xT4": 15,
    "projK1": 0, "projV1": 0, "projK4": 9, "projV2": 14, "tapW": 14, "ffn0": 81, "ffn1": 94, "ffn2": 99, "ffn3": 109,
}


LATER = {
    ("apply0", 0): 1, ("apply0", 1): 1, ("apply0", 3): -1, ("apply2", 1): -1, ("apply3", 3): 1, ("apply4", 2): -1,
    ("apply4", 3): -1, ("bd2", 2): 1, ("experts", 1): -1, ("gate", 0): 1, ("gate", 1): -1, ("gatedT", 1): -1,
    ("projP", 1): -1, ("projQ1", 0): 1, ("projQ1", 1): 1, ("projQ4", 0): 1, ("projQ4", 2): 1, ("retY", 1): 2,
    ("route", 1): -1, ("rstd0", 0): 1, ("rstd2", 1): -1, ("rstd3", 0): 1, ("rstd3", 3): 1, ("rstd4", 1): 1,
    ("rstd4", 2): -1, ("rstd4", 3): -1, ("silu", 2): 1, ("taps", 1): -1, ("xT0", 0): 1, ("xT1", 1): -1,
    ("xT2", 1): -1, ("xT3", 3): 1, ("xT4", 2): 1, ("xT4", 3): -1,
}


def place(kind, j):
    return PLACE[kind] + LATER.get((kind, j), 0)


def make_schedule():
    at = {}

    def put(slot, *item):
        at.setdefault((slot // UNITS, slot % UNITS), []).append(item)

    def norm(n, j, start):
        for kind in ("rstd", "apply", "xT"):
            put(start + place(f"{kind}{n}", j), kind, n, j)

    for k, (core, j) in enumerate(STEPS):
        start = UNITS * k
        if core == RET:
            for e in range(2):
                put(start + GROUPS * e + PLACE["grab"], "grab", 2 * j + e)
            for kind in ("center", "spread", "retY"):
                put(start + place(kind, j), kind, j)
            norm(4, j, start)
            continue
        for e in range(2):
            for kind in ("recip", "rT", "outT", "y"):
                put(start + GROUPS * e + PLACE[kind], kind, core, 2 * j + e)
        norm(core, j, start)
        if core == A0:
            put(start + place("projQ1", j), "projQ1", j)
            put(start + place("bd1", j), "bd", A1, j)
            continue
        for kind in ("route", "gate", "gatedT", "experts"):
            put(start + place(kind, j), kind, j)
        norm(2, j, start)
        put(start + place("projP", j), "projP", j)
        for c in range(CHUNKS):
            put(start + place("taps", j) + c, "taps", j, c)
        put(start + place("memY", j), "memY", j)
        norm(3, j, start)
        put(start + place("projQ4", j), "projQ4", j)
        put(start + place("bd2", j), "bd", RET, j)
        put(start + place("silu", j), "silu", j)
    for h in range(2):
        put(PLACE["projK1"] + h, "projK", 1, h)
        put(PLACE["projV1"] + h, "projV", 1, h)
        put(PLACE["projK4"] + h, "projK4", h)
        put(PLACE["projV2"] + h, "projV", 2, h)
        put(PLACE["tapW"] + h, "tapW", h)
    ends = {}
    for j in (0, 1):
        slot = PLACE[f"ffn{j}"]
        for layer in range(3):
            for m in range(ffn_parts(layer)):
                put(slot, "ff", j, layer, m)
                slot += 1
        ends[j] = slot
    slot = PLACE["ffn2"]
    for layer in range(3):
        for j in (2, 3):
            if (layer, j) == (0, 3):
                slot = max(slot, PLACE["ffn3"])
            for m in range(ffn_parts(layer)):
                put(slot, "ff", j, layer, m)
                slot += 1
    ends[2], ends[3] = slot, slot + 1
    for j, slot in ends.items():
        put(slot, "ffY", j)
        put(slot, "rstd", 5, j)
        put(slot + (j < 3), "apply", 5, j)
    return {place: sorted(items, key=lambda item: item[0] == "taps") for place, items in at.items()}


def ffn_parts(layer):
    return KT if layer == 0 else KT // 2


PROLOGUE = [("projK", 0, 0), ("bd", A0, 0), ("projQ0", 0), ("bd", A0, 1), ("projV", 0, 0),
            ("projK", 0, 1), ("bd", A0, 2), ("bd", A0, 3), ("projQ0", 1), ("projV", 0, 1)]
MISC_USES = dict(rT=1, y=1, xT=1, projQ1=1, projK=1, projV=1, projK4=2, projQ0=1, route=1, gatedT=1, experts=1,
                 projP=1, memY=1, projQ4=2, silu=1, center=1, spread=1, retY=1, ffY=1, taps=1)
TAPS_DONE = 2 * DVE_TAPS + CHUNKS
WALK_STEPS = CORE_STEPS + 5


def build(nc, t):
    schedule = make_schedule()
    order = [*PROLOGUE]
    for k in range(WALK_STEPS):
        for v in range(UNITS):
            order += schedule.get((k, v), [])
    misc_at, n = {}, 0
    for item in order:
        misc_at[item] = n
        n += MISC_USES.get(item[0], 0)
    n_misc = n

    with ExitStack() as ctx:
        def sb(name, shape, dt=F32):
            return ctx.enter_context(nc.sbuf_tensor(name, shape, dt))

        def sem(name):
            return ctx.enter_context(nc.semaphore(name))

        X = sb("X", [128, B, D])
        XB = sb("XB", [128, B, D])
        Z = sb("Z", [128, B, D])
        wh = sb("wh", [128, 2, KT, HID])
        early = wh[:, :, :, :].rearrange("p a b c -> p (a b c)")
        kT = early[:, 0:2 * B * S].rearrange("p (c n) -> p c n", c=2)
        maskI = early[:, 2 * B * S:3 * B * S].bitcast(I32).rearrange("p (b s) -> p b s", b=B)
        xT0 = early[:, 3 * B * S:4 * B * S]
        ctxT = sb("ctxT", [128, B * S])
        gT = sb("gT", [128, B, S])
        maskHi = sb("maskHi", [128, B, S], BF16)
        maskLo = sb("maskLo", [128, B, S], BF16)
        bd = sb("bd", [128, B, H, S])
        vpad = sb("vpad", [128, 2, H, COLG])
        vals = sb("vals", [128, 3, B, D])
        statT = sb("statT", [128, 3, B * S])
        stat = sb("stat", [128, 2, S])
        probs = sb("probs", [128, 3, HG * S])
        weightsT = sb("weightsT", [128, 3, HG, S])
        nmax = sb("nmax", [128, UNITS, HG])
        rowsum = sb("rowsum", [128, 2, H])
        recip = sb("recip", [128, 2, H])
        rexp = sb("rexp", [128, 2, H, DH])
        rTs = sb("rTs", [128, 2, S])
        outT = sb("outT", [128, 2, S])
        st6 = sb("st6", [128, 2, 6])
        mv = sb("mv", [128, 5, B, 2])
        nmean = sb("nmean", [128, 5, B])
        nmr = sb("nmr", [128, 5, B])
        vpe = sb("vpe", [128, 5, B])
        rstd = sb("rstd", [128, 5, B])
        mhalf = sb("mhalf", [128, 1])
        xTs = sb("xTs", [128, 4, 2 * S])
        lg = sb("lg", [128, 2, E_])
        top = sb("top", [128, 2, 8])
        lsub = sb("lsub", [128, 2, E_])
        lexp = sb("lexp", [128, 2, E_])
        keep = sb("keep", [128, 2, E_])
        kept = sb("kept", [128, 2, E_])
        esum = sb("esum", [128, 2])
        erec = sb("erec", [128, 2])
        wexp = sb("wexp", [128, 2, E_])
        gated = sb("gated", [128, 2, E_, R_])
        gatedT = sb("gatedT", [128, 2 * S])
        axs = sb("axs", [128, 2, E_, R_])
        PADW = TAPS - 1 + S
        pPad = sb("pPad", [128, 2, 2, PADW])
        ptime = sb("ptime", [128, 2, 2])
        pfar = sb("pfar", [128, 2, 2])
        mem = ctxT[:, 0:4 * S].rearrange("p (a b s) -> p a b s", a=2, b=2)
        memP = sb("memP", [128, 2, 2, S])
        tapW = sb("tapW", [128, PE_TAPS, 128])
        prod = sb("prod", [128, PRODUCTS, 2, S])
        mwd = sb("mwd", [128, TAPS])
        qa = sb("qa", [128, 2, S])
        qb = sb("qb", [128, 2, S])
        q4T = statT[:, 1, :]
        silu = vals[:, 0, :, :].rearrange("p b d -> p (b d)")
        ret = sb("ret", [128, 2, 2 * S])
        cen = ctxT[:, 4 * S:8 * S].rearrange("p (a n) -> p a n", a=2)
        sq = sb("sq", [128, 2 * S])
        sd = sb("sd", [128, 2 * S])
        rsd = sb("rsd", [128, 2 * S])
        rg = sb("rg", [128, 2 * S])
        rg2 = sb("rg2", [128, 2 * S])
        causalT = sb("causalT", [128, S])
        bdw = bd[:, :, :, :].rearrange("p b h s -> p (b h s)")
        hid = [bdw[:, n * 2048:(n + 1) * 2048].rearrange("p (a m s) -> p a m s", a=2, m=KT) for n in range(3)]
        gateA = probs[:, :, 0:2 * S]
        ysc = sb("ysc", [128, 2, D])
        x5T = statT[:, 0, :].rearrange("p (j n) -> p j n", j=PAIRS)
        w0 = sb("w0", [128, 4, 128])
        w1 = sb("w1", [128, 4, 128])
        wr = sb("wr", [128, 7, 128])
        wm = sb("wm", [128, 2 * 128 + 128 + E_])
        wf = sb("wf", [128, 2, 128])
        wi = gT[:, :, :].rearrange("p b s -> p (b s)").rearrange("p (i n) -> p i n", i=2)
        wo3 = maskHi[:, :, :].rearrange("p b s -> p (b s)").bitcast(F32).rearrange("p (k n) -> p k n", k=KT)
        cols = sb("cols", [128, NCOLS])
        rows = sb("rows", [128, len(ROWS), 128])
        rbr = sb("rbr", [128, E_])
        bqs = sb("bqs", [128, 2])
        ident = sb("ident", [128, 128])
        mats = sb("mats", [128, 2, 128])
        xpos = sb("xpos", [128, 4, 128])
        bfc = sb("bfc", [128, 3, 128], BF16)
        epsc = sb("epsc", [128, 1])

        ps = ctx.enter_context(nc.psum_tensor("ps", [128, 8, 512], F32))
        probsT_ps = ps[:, 2, :]
        out_ps = [ps[:, 4, 0:S], ps[:, 5, 0:S]]
        misc_ps = [ps[:, 6, :], ps[:, 7, :]]

        ld = {name: sem(f"loaded_{name}") for name in t if name != "out"}
        zeroed_bd = [sem(f"zeroed_bd{j}") for j in range(PAIRS)]
        zeroed_vpad = sem("zeroed_vpad")
        consts = sem("consts_ready")
        masks = sem("masks_ready")
        scores = sem("scores")
        negmax = sem("negmax")
        probs_ready = sem("probs_ready")
        probsT = sem("probsT")
        wT = sem("weightsT_ready")
        pv = sem("pv")
        stat_ready = sem("stat_ready")
        vpad_ready = sem("vpad_ready")
        recip_ready = sem("recip_ready")
        rexp_ready = sem("rexp_ready")
        rTs_ready = sem("rTs_ready")
        out_taken = sem("out_taken")
        misc_ready = [sem(f"misc_ready{n}") for n in range(2)]
        z_ready = sem("z_ready")
        routed = sem("routed")
        k4_cos, k4_sin = sem("k4_cos"), sem("k4_sin")
        q4_cos, q4_sin = sem("q4_cos"), sem("q4_sin")
        bd_ready = [[sem(f"bd_ready{j}_{g}") for g in range(GROUPS)] for j in range(PAIRS)]
        kT_ready = [sem("kT0_ready"), sem("kT1_ready")]
        q4_ready = sem("q4T_ready")
        statT_ready = [sem(f"statT{n}_ready") for n in range(3)]
        vals_ready = [sem(f"vals{n}_ready") for n in range(3)]
        mv_ready = sem("variance_ready")
        rstd_ready = sem("rstd_ready")
        x_ready = sem("x_ready")
        xb_ready = sem("xb_ready")
        xTs_ready = sem("xTs_ready")
        lsub_ready = sem("lsub_ready")
        lexp_ready = sem("lexp_ready")
        gated_ready = sem("gated_ready")
        gatedT_ready = sem("gatedT_ready")
        p_ready = sem("p_ready")
        pads = sem("pads_ready")
        taps_done = sem("taps_done")
        tapW_ready = sem("tapW_ready")
        products = sem("products")
        pool_taps = sem("pool_taps")
        silu_ready = sem("silu_ready")
        ret_ready = sem("ret_ready")
        cen_ready = sem("cen_ready")
        sq_ready = sem("sq_ready")
        sd_ready = sem("sd_ready")
        rg_ready = sem("rg_ready")
        hid_ps = sem("hidden_in_psum")
        gateA_ready = sem("gateA_ready")
        hid_ready = [sem(f"hidden{n}_ready") for n in range(3)]
        y_free = sem("ffn_y_free")
        out_done = sem("out_done")
        dve_own = sem("dve_own")
        pool_own = sem("pool_own")

        block = ctx.enter_context(nc.Block())

        def scores_ps(u):
            return ps[:, (0, 1, 3)[u % 3] if u < SOFTMAX_UNITS else (1, 0)[u % 2], :]

        def misc(item, n=0):
            at = misc_at[item] + n
            return misc_ps[at % 2], at % 2, at // 2

        def wait_misc(engine, item, n=0):
            _, i, before = misc(item, n)
            engine.wait_ge(misc_ready[i], before + 1)

        def bcast(ap, n):
            return ap.unsqueeze(1).broadcast_to([128, n, ap.shape[-1]])

        def inner(ap, n):
            return ap.unsqueeze(2).broadcast_to([128, ap.shape[-1], n])

        def col(name, n=0):
            return cols[:, COLS[name] + n:COLS[name] + n + 1]

        def row(name):
            return rows[:, ROWS[name], :]

        def pair(tensor, j):
            return tensor[:, 2 * S * j:2 * S * (j + 1)]

        def norm_no(n, j):
            return norm_at[(n, j)]

        norm_at = {}
        for item in order:
            if item[0] == "rstd":
                norm_at[item[1:]] = len(norm_at)

        def xT_no(n, j):
            return [i[1:] for i in order if i[0] == "xT"].index((n, j))

        def split_taps(first, n, c):
            return range(first + n * c // CHUNKS, first + n * (c + 1) // CHUNKS)

        def walk():
            for k in range(WALK_STEPS):
                for v in range(UNITS):
                    yield k, v, schedule.get((k, v), [])

        LAST = UNITS * CORE_STEPS
        bias_of = {0: "bo1", 1: "base_b", 2: "bias2", 3: "out_b"}

        reader, z_seen = [], 0
        for item in order:
            kind, arg = item[0], item[1:]
            if kind == "projK":
                reader.append((kT_ready[arg[0]], arg[1] + 1))
            elif kind == "projQ0":
                reader.append((statT_ready[0], arg[0] + 1))
            elif kind == "projV":
                reader.append((vals_ready[arg[0]], arg[1] + 1))
            elif kind == "projK4":
                reader += [(k4_cos, arg[0] + 1), (k4_sin, arg[0] + 1)]
            elif kind == "projQ1":
                reader.append((statT_ready[1], arg[0] + 1))
            elif kind == "rT":
                reader.append((rTs_ready, seq_no(*arg) + 1))
            elif kind == "y":
                z_seen += 1
                reader.append((z_ready, z_seen))
            elif kind == "xT":
                reader.append((xTs_ready, xT_no(*arg) + 1))
            elif kind == "route":
                reader.append((routed, arg[0] + 1))
            elif kind == "gatedT":
                reader.append((gatedT_ready, arg[0] + 1))
            elif kind in ("experts", "memY", "retY"):
                z_seen += 2
                reader.append((z_ready, z_seen))
            elif kind == "projP":
                reader.append((p_ready, arg[0] + 1))
            elif kind == "projQ4":
                reader += [(q4_cos, arg[0] + 1), (q4_sin, arg[0] + 1)]
            elif kind == "silu":
                reader.append((silu_ready, arg[0] + 1))
            elif kind == "center":
                reader.append((cen_ready, arg[0] + 1))
            elif kind == "spread":
                reader.append((sd_ready, arg[0] + 1))
            elif kind == "taps":
                reader.append((taps_done, TAPS_DONE * arg[0] + 2 * (DVE_TAPS * (arg[1] + 1) // CHUNKS) + arg[1] + 1))
            elif kind == "ffY":
                z_seen += 2
                reader.append((y_free, arg[0] + 1))
        misc_total = len(reader)
        assert misc_total == n_misc
        for kind in ("apply", "xT"):
            seen = [i[1:] for i in order if i[0] == kind]
            want = [i[1:] for i in order if i[0] == "rstd" and (kind == "apply" or i[1] < 5)]
            assert seen == want, (kind, seen, want)

        ffn_no, ffn_at, ffn_before, last_in, turn = {}, [], [], {}, 0
        for k in range(WALK_STEPS):
            for v in range(UNITS):
                for item in schedule.get((k, v), []):
                    if item[0] != "ff":
                        continue
                    n = ffn_no[item[1:]] = len(ffn_at)
                    ring = (2, 3) if (k, v) < (CORE_STEPS, 5) else (2, 3, 0, 1, 4, 5)
                    bank = ring[turn % len(ring)]
                    turn += 1
                    ffn_at.append(bank)
                    ffn_before.append(last_in.get(bank))
                    last_in[bank] = item[1:]

        def ffn_ps(item):
            return ps[:, ffn_at[ffn_no[item]], :]

        def hid_reader(item):
            j, layer, m = item
            return hid_ready[layer], ffn_parts(layer) * j + m + 1

        xb_at = {}
        for j in range(PAIRS):
            xb_at[(0, j)] = len(xb_at)
        for item in order:
            if item[0] == "apply" and item[1] in bias_of:
                xb_at[(item[1] + 1, item[2])] = len(xb_at)

        def xb_before(n, j):
            return xb_at[(n, j)] + 1

        def norm_rstd(n, j, pool):
            m = n if n < 5 else 0
            pool.wait_ge(mv_ready, norm_no(n, j) + 1)
            pool.tensor_tensor(rstd[:, m, 2 * j:2 * j + 2], vpe[:, m, 2 * j:2 * j + 2], mhalf[:, :].broadcast_to([128, 2]),
                               ALU.pow).then_inc(pool_own, 1)
            pool.wait_ge(pool_own, norm_no(n, j) + 1)
            pool.tensor_tensor(nmr[:, m, 2 * j:2 * j + 2], nmean[:, m, 2 * j:2 * j + 2], rstd[:, m, 2 * j:2 * j + 2],
                               ALU.mult).then_inc(rstd_ready, 1)

        @block.sync
        def _(sp):
            for name, dst in (("w0", w0[:, :, :]), ("xT0", xT0[:, :]), ("cols", cols[:, :]), ("bfc", bfc[:, :, :]),
                              ("rows", rows[:, :, :]), ("ident", ident[:, :]), ("ctxT", ctxT[:, :]), ("w1", w1[:, :, :]),
                              ("X", X[:, :, :]), ("maskI", maskI[:, :, :]), ("gT", gT[:, :, :]), ("wr", wr[:, :, :]),
                              ("xpos", xpos[:, :, :])):
                sp.dma_start(dst, t[name]).then_inc(ld[name], 16)

            def spread_heads(core, j):
                sp.wait_ge(zeroed_bd[j], 1)
                if core == RET:
                    sp.wait_ge(q4_ready, j + 1)
                    src = q4T
                else:
                    sp.wait_ge(kT_ready[core], j // 2 + 1)
                    src = kT[:, core, :]
                if core > A0:
                    sp.wait_ge(scores, UNITS * (STEP_OF[core - 1, j] + 1))
                for n in range(H):
                    g, i = n // HG, n % HG
                    h = head_of(g, i)
                    p = slice(DH * h, DH * (h + 1))
                    s_ = (src[p, 2 * S * j:2 * S * (j + 1)]).rearrange("p (b s) -> p b s", b=2)
                    sp.dma_start(bd[p, 2 * j:2 * j + 2, n, :], s_).then_inc(bd_ready[j][g], 16)

            for item in PROLOGUE:
                if item[0] == "bd":
                    spread_heads(*item[1:])
            for name, dst in (("wm", wm[:, :]), ("rbr", rbr[:, :]), ("wf", wf[:, :, :]), ("causalT", causalT[:, :]),
                              ("mats", mats[:, :, :])):
                sp.dma_start(dst, t[name]).then_inc(ld[name], 16)
            for k, v, items in walk():
                for item in items:
                    if item[0] == "bd":
                        spread_heads(*item[1:])
                    if item[:2] == ("apply", 5):
                        j = item[2]
                        sp.wait_ge(x_ready, norm_no(5, j) + 1)
                        sp.dma_start(t["out"][:, 2 * j:2 * j + 2, :], X[:, 2 * j:2 * j + 2, :]).then_inc(out_done, 16)
                if (k, v) == (STEP_OF[A0, 3] + 1, 2):
                    for groups in bd_ready:
                        for n in groups:
                            sp.wait_ge(n, 16 * HG * 2)
                    sp.wait_ge(masks, 1)
                    sp.wait_ge(vals_ready[0], 2)
                    sp.wait_ge(statT_ready[0], 2)
                    sp.dma_start(wh[:, :, :, :], t["wh"]).then_inc(ld["wh"], 16)
                if (k, v) == (2 * PAIRS, 2):
                    sp.wait_ge(wT, SOFTMAX_UNITS)
                    sp.wait_ge(scores, SOFTMAX_UNITS)
                    sp.dma_start(wi[:, :, :], t["wi"]).then_inc(ld["wi"], 16)
                    sp.dma_start(wo3[:, :, :], t["wo3"]).then_inc(ld["wo3"], 16)
            sp.wait_ge(out_done, 16 * PAIRS)

        @block.gpsimd
        def _(pool):
            pool.memset(mhalf[:, :], -0.5)
            pool.memset(epsc[:, :], EPS)
            pool.memset(pPad[:, :, :, :], 0.0).then_inc(pads, 1)
            for j in (2, 3):
                pool.memset(bd[:, 2 * j:2 * j + 2, :, :], 0.0).then_inc(zeroed_bd[j], 1)

            def stage_in(core, j, e):
                b, n = 2 * j + e, 2 * STEP_OF[core, j] + e
                if n >= 2:
                    pool.wait_ge(scores, GROUPS * (n - 1))
                pool.wait_ge(statT_ready[core], b // 4 + 1 if core != A1 else j + 1)
                pool.tensor_copy(stat[:, e, :], statT[:, core, S * b:S * (b + 1)]).then_inc(stat_ready, 1)
                if n >= 2:
                    pool.wait_ge(pv, GROUPS * (n - 1))
                else:
                    pool.wait_ge(zeroed_vpad, 1)
                pool.wait_ge(vals_ready[core], b // 4 + 1)
                blocks = vpad[:, e, :, :].rearrange("p h d -> p (h d)")
                diag = bass_diag(blocks)
                pool.tensor_copy(diag, vals[:, core, b, :].rearrange("p (i g d) -> p i g d", i=HG, g=GROUPS)).then_inc(vpad_ready, 1)

            def bass_diag(flat):
                return bass.AP(flat.tensor, flat.offset, [list(flat.ap[0]), [GROUPS * COLG, HG], [COLG + DH, GROUPS], [1, DH]])

            stage_in(A0, 0, 0)
            pool.wait_ge(ld["X"], 16)
            pool.wait_ge(ld["rows"], 16)
            for b in range(0, B, 2):
                pool.tensor_tensor(XB[:, b:b + 2, :], X[:, b:b + 2, :], bcast(row("bo0"), 2), ALU.add).then_inc(xb_ready, 1)
            for k, v, items in walk():
                nxt = None
                if v == 0 and k < CORE_STEPS:
                    nxt = (*STEPS[k], 1)
                if v == 4 and k + 1 < CORE_STEPS:
                    nxt = (*STEPS[k + 1], 0)
                if nxt:
                    stage_in(*nxt)
                for item in items:
                    if item[0] == "recip":
                        c, b = item[1:]
                        n = seq_no(c, b)
                        pool.wait_ge(recip_ready, n + 1)
                        if n >= 2:
                            core, b_, _, _ = unit(GROUPS * (n - 2))
                            wait_misc(pool, ("rT", core, b_))
                        pool.tensor_copy(rexp[:, b % 2, :, :], inner(recip[:, b % 2, :], DH)).then_inc(rexp_ready, 1)
                    if item[0] == "taps":
                        j, c = item[1:]
                        for i in split_taps(TAPS - POOL_TAPS, POOL_TAPS, c):
                            if i == TAPS - POOL_TAPS:
                                continue
                            n = i - (TAPS - POOL_TAPS) + POOL_TAPS * j
                            pool.wait_ge(products, n - j)
                            pool.wait_ge(pool_taps, n)
                            pool.tensor_tensor(memP[:, j % 2, :, :], memP[:, j % 2, :, :], prod[:, n % PRODUCTS, :, :],
                                               ALU.add).then_inc(pool_taps, 1)
                    if item[0] == "rstd":
                        norm_rstd(item[1], item[2], pool)
                    if item[0] == "apply" and item[1] in bias_of:
                        n, j = item[1:]
                        pool.wait_ge(x_ready, norm_no(n, j) + 1)
                        pool.tensor_tensor(XB[:, 2 * j:2 * j + 2, :], X[:, 2 * j:2 * j + 2, :], bcast(row(bias_of[n]), 2),
                                           ALU.add).then_inc(xb_ready, 1)

        @block.scalar
        def _(act):
            def ready(item, n=0):
                bank, i, before = misc(item, n)
                act.wait_ge(misc_ready[i], before + 1)
                return bank

            def exps(u):
                core, b, g, e = unit(u)
                act.wait_ge(negmax, u + 1)
                if u >= 3:
                    act.wait_ge(probsT, u - 2)
                for i in range(HG):
                    last = act.activation(probs[:, u % 3, S * i:S * (i + 1)], scores_ps(u)[:, S * i:S * (i + 1)], ACT.Exp,
                                          bias=nmax[:, u % UNITS, i:i + 1],
                                          accum_out=rowsum[:, e, head_of(g, i):head_of(g, i) + 1])
                last.then_inc(probs_ready, 1)

            def run(item):
                kind, arg = item[0], item[1:]
                if kind == "projK":
                    c, h = arg
                    bank = ready(item)
                    act.activation(kT[:, c, 512 * h:512 * (h + 1)], bank, ACT.Identity,
                                   bias=col("bk0" if c == 0 else "bk1")).then_inc(kT_ready[c], 1)
                elif kind == "projQ0":
                    h, = arg
                    bank = ready(item)
                    act.wait_ge(consts, 1)
                    act.activation(statT[:, 0, 512 * h:512 * (h + 1)], bank, ACT.Identity, bias=bqs[:, 0:1],
                                   scale=SCALE).then_inc(statT_ready[0], 1)
                elif kind == "projQ1":
                    j, = arg
                    bank = ready(item)
                    act.activation(pair(statT[:, 1, :], j), bank[:, 0:2 * S], ACT.Identity, bias=bqs[:, 1:2],
                                   scale=SCALE).then_inc(statT_ready[1], 1)
                elif kind == "rT":
                    c, b = arg
                    bank = ready(item)
                    n = seq_no(c, b)
                    if n >= 2:
                        act.wait_ge(out_taken, n - 1)
                    act.copy(rTs[:, b % 2, :], bank[:, 0:S]).then_inc(rTs_ready, 1)
                elif kind == "xT":
                    n, j = arg
                    bank = ready(item)
                    act.copy(xTs[:, n, :] if n < 4 else x5T[:, j, :], bank[:, 0:2 * S]).then_inc(xTs_ready, 1)
                elif kind == "apply":
                    n, j = arg
                    m = n if n < 5 else 0
                    act.wait_ge(rstd_ready, norm_no(n, j) + 1)
                    if n < 5:
                        act.wait_ge(xb_ready, xb_before(n, j))
                    for b in (2 * j, 2 * j + 1):
                        last = act.activation(X[:, b, :], Z[:, b, :], ACT.Identity, bias=nmr[:, m, b:b + 1],
                                              scale=rstd[:, m, b:b + 1])
                    last.then_inc(x_ready, 1)
                elif kind == "gate":
                    j, = arg
                    act.wait_ge(lsub_ready, j + 1)
                    act.activation(lexp[:, :, :], lsub[:, :, :], ACT.Exp).then_inc(lexp_ready, 1)
                elif kind == "gatedT":
                    j, = arg
                    bank = ready(item)
                    act.copy(gatedT[:, :], bank[:, 0:2 * S]).then_inc(gatedT_ready, 1)
                elif kind == "projP":
                    j, = arg
                    bank = ready(item)
                    act.wait_ge(pads, 1)
                    if j >= 2:
                        act.wait_ge(taps_done, TAPS_DONE * (j - 1))
                    for e in range(2):
                        last = act.activation(pPad[:, j % 2, e, TAPS - 1:PADW], bank[:, S * e:S * (e + 1)], ACT.Identity,
                                              bias=col("bias1"), accum_out=ptime[:, j % 2, e:e + 1])
                    last.then_inc(p_ready, 1)
                elif kind == "tapW":
                    h, = arg
                    act.wait_ge(ld["ident"], 16)
                    act.wait_ge(consts, 2)
                    for n in range(PE_TAPS * h // 2, PE_TAPS * (h + 1) // 2):
                        last = act.activation(tapW[:, n, :], ident[:, :], ACT.Copy, scale=mwd[:, DVE_TAPS + n:DVE_TAPS + n + 1])
                    last.then_inc(tapW_ready, 1)
                elif kind == "taps":
                    j, c = arg
                    for i in split_taps(TAPS - POOL_TAPS, POOL_TAPS, c):
                        n = i - (TAPS - POOL_TAPS) + POOL_TAPS * j
                        src = pPad[:, j % 2, :, TAPS - 1 - i:TAPS - 1 - i + S]
                        if i == TAPS - POOL_TAPS:
                            act.wait_ge(p_ready, j + 1)
                            act.wait_ge(consts, 2)
                            if j >= 2:
                                wait_misc(act, ("memY", j - 2))
                            if j >= 1:
                                act.wait_ge(pool_taps, n)
                            act.activation(memP[:, j % 2, :, :], src, ACT.Copy, scale=mwd[:, i:i + 1]).then_inc(pool_taps, 1)
                        else:
                            if n >= PRODUCTS:
                                act.wait_ge(pool_taps, n - PRODUCTS + 1)
                            act.activation(prod[:, n % PRODUCTS, :, :], src, ACT.Copy, scale=mwd[:, i:i + 1]).then_inc(products, 1)
                elif kind == "silu":
                    j, = arg
                    bank = ready(item)
                    act.activation(pair(silu, j), bank[:, 0:2 * S], ACT.Silu, bias=col("gb")).then_inc(silu_ready, 1)
                elif kind == "center":
                    j, = arg
                    bank = ready(item)
                    if j >= 2:
                        act.wait_ge(rg_ready, j - 1)
                    act.copy(cen[:, j % 2, :], bank[:, 0:2 * S]).then_inc(cen_ready, 1)
                elif kind == "spread":
                    j, = arg
                    bank = ready(item)
                    act.wait_ge(pads, 1)
                    if j >= 1:
                        act.wait_ge(rg_ready, j)
                    act.activation(sd[:, :], bank[:, 0:2 * S], ACT.Sqrt, bias=epsc[:, :]).then_inc(sd_ready, 1)
                elif kind == "ff":
                    j, layer, m = arg
                    act.wait_ge(hid_ps, ffn_no[arg] + 1)
                    if layer == 0:
                        if KT * j + m >= 2:
                            act.wait_ge(hid_ready[0], KT * j + m - 1)
                        else:
                            act.wait_ge(probsT, SOFTMAX_UNITS)
                        act.activation(gateA[:, m % 2, :], ffn_ps(arg)[:, 0:2 * S], ACT.Silu,
                                       scale=col("s1", m)).then_inc(gateA_ready, 1)
                    else:
                        if j >= 2 and m == 0:
                            if layer == 1:
                                act.wait_ge(hid_ps, ffn_no[(j - 2, 2, 1)] + 1)
                            else:
                                wait_misc(act, ("ffY", j - 2))
                        if j < 2:
                            act.wait_ge(scores, UNITS * (STEP_OF[RET, layer - 1] + 1))
                        for half in range(2):
                            last = act.activation(hid[layer][:, j % 2, 2 * m + half, :],
                                                  ffn_ps(arg)[:, 2 * S * half:2 * S * (half + 1)], ACT.Gelu,
                                                  scale=col("sh1" if layer == 1 else "sh2", 2 * m + half))
                        last.then_inc(hid_ready[layer], 1)

            act.memzero(vpad[:, :, :, :]).then_inc(zeroed_vpad, 1)
            act.wait_ge(ld["cols"], 16)
            for item in PROLOGUE:
                run(item)
            exps(0)
            exps(1)
            for k, v, items in walk():
                u = UNITS * k + v
                for item in items:
                    run(item)
                if u + 2 < SOFTMAX_UNITS:
                    exps(u + 2)

        @block.vector
        def _(dve):
            own = [0]
            z_count = [0]
            tap_count = [0]

            def link(ins):
                own[0] += 1
                ins.then_inc(dve_own, 1)
                dve.wait_ge(dve_own, own[0])

            def ready(item, n=0):
                bank, i, before = misc(item, n)
                dve.wait_ge(misc_ready[i], before + 1)
                return bank

            def row_max(u):
                dve.wait_ge(scores, u + 1)
                dve.tensor_reduce(nmax[:, u % UNITS, :], scores_ps(u).rearrange("p (h k) -> p h k", h=HG), AX.X,
                                  ALU.max, negate=True).then_inc(negmax, 1)

            def take_weights(u):
                core, b, _, _ = unit(u)
                dve.wait_ge(probsT, u + 1)
                if u >= 3:
                    dve.wait_ge(pv, u - 2)
                src = probsT_ps.rearrange("p (h q) -> p h q", h=HG)
                if core == A0:
                    dve.tensor_copy(weightsT[:, u % 3, :, :], src).then_inc(wT, 1)
                else:
                    if u == UNITS * STEP_OF[A1, 0]:
                        dve.wait_ge(ld["gT"], 16)
                    dve.tensor_tensor(weightsT[:, u % 3, :, :], src, bcast(gT[:, b, :], HG), ALU.mult).then_inc(wT, 1)

            def decay(u):
                g = u % GROUPS
                dve.wait_ge(scores, u + 1)
                if u == 16 * GROUPS:
                    dve.wait_ge(ld["causalT"], 16)
                dve.wait_ge(pv, u - 2)
                dve.tensor_tensor(weightsT[:, u % 3, :, :], scores_ps(u).rearrange("p (h q) -> p h q", h=HG),
                                  bcast(causalT[:, :], HG), ALU.mult).then_inc(wT, 1)

            def stats(n, sequences, last_op):
                m = n if n < 5 else 0
                z_count[0] += len(sequences)
                last_op.then_inc(z_ready, len(sequences))
                dve.wait_ge(z_ready, z_count[0])
                for b in sequences:
                    last = dve.bn_stats(st6[:, b % 2, :], Z[:, b, :])
                link(last)
                for b in sequences:
                    last = dve.bn_aggr(mv[:, m, b, :], st6[:, b % 2, :])
                link(last)

            def add_eps(n, j):
                m = n if n < 5 else 0
                dve.tensor_scalar(vpe[:, m, 2 * j:2 * j + 2], mv[:, m, 2 * j:2 * j + 2, 1], EPS, None, ALU.add)
                dve.tensor_scalar(nmean[:, m, 2 * j:2 * j + 2], mv[:, m, 2 * j:2 * j + 2, 0], -1.0, None, ALU.mult).then_inc(mv_ready, 1)

            def add_pair(n, j, bank):
                dve.wait_ge(xb_ready, xb_before(n, j))
                stats(n, (2 * j, 2 * j + 1), dve.tensor_tensor(
                    Z[:, 2 * j:2 * j + 2, :], bank[:, 0:2 * D].rearrange("p (e d) -> p e d", e=2),
                    XB[:, 2 * j:2 * j + 2, :], ALU.add))

            def run(item):
                kind, arg = item[0], item[1:]
                if kind == "projV":
                    c, h = arg
                    bank = ready(item)
                    src = bank.rearrange("p (b d) -> p b d", b=4)
                    dst = vals[:, c, 4 * h:4 * h + 4, :]
                    if c == RET:
                        ins = dve.tensor_copy(dst, src)
                    else:
                        dve.wait_ge(ld["rows"], 16)
                        ins = dve.tensor_tensor(dst, src, bcast(row("bv0" if c == 0 else "bv1"), 4), ALU.add)
                    ins.then_inc(vals_ready[c], 1)
                elif kind == "projK4":
                    h, = arg
                    dst = statT[:, 2, 512 * h:512 * (h + 1)].rearrange("p (b s) -> p b s", b=4)
                    dve.wait_ge(ld["xpos"], 16)
                    bank = ready(item)
                    dve.tensor_tensor(dst, bank.rearrange("p (b s) -> p b s", b=4), bcast(xpos[:, 2, :], 4), ALU.mult).then_inc(k4_cos, 1)
                    bank = ready(item, 1)
                    if h:
                        dve.wait_ge(statT_ready[2], h)
                    for i, tmp in enumerate((qa, qb)):
                        last = dve.tensor_tensor(tmp[:, :, :], bank[:, 2 * S * i:2 * S * (i + 1)].rearrange("p (b s) -> p b s", b=2),
                                                 bcast(xpos[:, 3, :], 2), ALU.mult)
                    last.then_inc(k4_sin, 1)
                    dve.wait_ge(k4_sin, h + 1)
                    for i, tmp in enumerate((qa, qb)):
                        last = dve.tensor_tensor(dst[:, 2 * i:2 * i + 2, :], dst[:, 2 * i:2 * i + 2, :], tmp[:, :, :], ALU.add)
                    last.then_inc(statT_ready[2], 1)
                elif kind == "recip":
                    c, b = arg
                    dve.wait_ge(probs_ready, GROUPS * (seq_no(c, b) + 1))
                    if seq_no(c, b) >= 2:
                        dve.wait_ge(rexp_ready, seq_no(c, b) - 1)
                    dve.reciprocal(recip[:, b % 2, :], rowsum[:, b % 2, :]).then_inc(recip_ready, 1)
                elif kind == "outT":
                    c, b = arg
                    n = seq_no(c, b)
                    dve.wait_ge(rTs_ready, n + 1)
                    dve.wait_ge(pv, GROUPS * (n + 1))
                    if n >= 2:
                        core, b_, _, _ = unit(GROUPS * (n - 2))
                        wait_misc(dve, ("y", core, b_))
                    dve.tensor_tensor(outT[:, b % 2, :], out_ps[b % 2], rTs[:, b % 2, :], ALU.mult).then_inc(out_taken, 1)
                elif kind == "y":
                    c, b = arg
                    bank = ready(item)
                    dve.wait_ge(xb_ready, xb_before(c, b // 2))
                    ins = dve.tensor_tensor(Z[:, b, :], bank[:, 0:D], XB[:, b, :], ALU.add)
                    stats(c, (b,), ins)
                elif kind == "rstd":
                    add_eps(*arg)
                elif kind == "route":
                    j, = arg
                    bank = ready(item)
                    dve.wait_ge(ld["rbr"], 16)
                    both = bank[:, 0:2 * (128 + E_)].rearrange("p (e n) -> p e n", e=2)
                    dve.tensor_tensor(lg[:, :, :], both[:, :, 128:], bcast(rbr[:, :], 2), ALU.add)
                    dve.tensor_copy(axs[:, :, :, :].rearrange("p a b c -> p a (b c)"), both[:, :, 0:128]).then_inc(routed, 1)
                    dve.wait_ge(routed, j + 1)
                    dve.max(top[:, 0, :], lg[:, 0, :])
                    link(dve.max(top[:, 1, :], lg[:, 1, :]))
                    dve.tensor_tensor(lsub[:, :, :], lg[:, :, :], inner(top[:, :, 0], E_), ALU.subtract).then_inc(lsub_ready, 1)
                    link(dve.tensor_tensor(keep[:, :, :], lg[:, :, :], inner(top[:, :, 1], E_), ALU.is_ge))
                elif kind == "gate":
                    j, = arg
                    dve.wait_ge(lexp_ready, j + 1)
                    link(dve.tensor_tensor(kept[:, :, :], keep[:, :, :], lexp[:, :, :], ALU.mult))
                    link(dve.tensor_reduce(esum[:, :], kept[:, :, :], AX.X, ALU.add))
                    link(dve.reciprocal(erec[:, :], esum[:, :]))
                    for e in range(2):
                        last = dve.tensor_scalar(wexp[:, e, :], kept[:, e, :], erec[:, e:e + 1], 2.0, ALU.mult, ALU.mult)
                    link(last)
                    for e in range(2):
                        last = dve.tensor_tensor(gated[:, e, :, :], axs[:, e, :, :], inner(wexp[:, e, :], R_), ALU.mult)
                    last.then_inc(gated_ready, 1)
                elif kind == "experts":
                    j, = arg
                    bank = ready(item)
                    add_pair(2, j, bank)
                elif kind == "taps":
                    j, c = arg
                    if c == 0:
                        dve.wait_ge(p_ready, j + 1)
                        if j == 0:
                            dve.wait_ge(consts, 2)
                        if j >= 2:
                            wait_misc(dve, ("memY", j - 2))
                        link(dve.tensor_scalar(pfar[:, j % 2, :], ptime[:, j % 2, :], col("mw"), None, ALU.mult))
                    else:
                        dve.wait_ge(taps_done, tap_count[0])
                    for i in split_taps(0, DVE_TAPS, c):
                        for e in range(2):
                            acc, src = mem[:, j % 2, e, :], pPad[:, j % 2, e, TAPS - 1 - i:TAPS - 1 - i + S]
                            if i == 0:
                                last = dve.tensor_scalar(acc, src, mwd[:, 0:1], pfar[:, j % 2, e:e + 1], ALU.mult, ALU.add)
                            else:
                                dve.wait_ge(taps_done, tap_count[0] - 1)
                                last = dve.scalar_tensor_tensor(acc, src, mwd[:, i:i + 1], acc, ALU.mult, ALU.add)
                            last.then_inc(taps_done, 1)
                            tap_count[0] += 1
                    bank = ready(item)
                    dve.wait_ge(taps_done, tap_count[0])
                    dve.tensor_tensor(mem[:, j % 2, :, :], mem[:, j % 2, :, :], bank[:, 0:2 * S].rearrange("p (e s) -> p e s", e=2),
                                      ALU.add).then_inc(taps_done, 1)
                    tap_count[0] += 1
                    if c == CHUNKS - 1:
                        assert tap_count[0] == TAPS_DONE * (j + 1)
                elif kind == "memY":
                    j, = arg
                    bank = ready(item)
                    add_pair(3, j, bank)
                elif kind == "projQ4":
                    j, = arg
                    bank = ready(item)
                    if j:
                        dve.wait_ge(q4_ready, j)
                    else:
                        dve.wait_ge(statT_ready[2], 2)
                    dve.tensor_tensor(qa[:, :, :], bank[:, 0:2 * S].rearrange("p (e s) -> p e s", e=2), bcast(xpos[:, 0, :], 2),
                                      ALU.mult).then_inc(q4_cos, 1)
                    bank = ready(item, 1)
                    dve.tensor_tensor(qb[:, :, :], bank[:, 0:2 * S].rearrange("p (e s) -> p e s", e=2),
                                      bcast(xpos[:, 1, :], 2), ALU.mult).then_inc(q4_sin, 1)
                    dve.wait_ge(q4_sin, j + 1)
                    dve.tensor_tensor(pair(q4T, j).rearrange("p (e s) -> p e s", e=2), qa[:, :, :], qb[:, :, :],
                                      ALU.add).then_inc(q4_ready, 1)
                elif kind == "grab":
                    b, = arg
                    n = 2 * B + b
                    dve.wait_ge(pv, GROUPS * (n + 1))
                    if b >= 4:
                        wait_misc(dve, ("center", b // 2 - 2))
                    dve.tensor_copy(ret[:, (b // 2) % 2, S * (b % 2):S * (b % 2 + 1)], out_ps[b % 2]).then_inc(out_taken, 1)
                elif kind == "center":
                    j, = arg
                    dve.wait_ge(cen_ready, j + 1)
                    if j >= 1:
                        wait_misc(dve, ("spread", j - 1))
                    dve.tensor_tensor(sq[:, :], cen[:, j % 2, :], cen[:, j % 2, :], ALU.mult).then_inc(sq_ready, 1)
                elif kind == "spread":
                    j, = arg
                    dve.wait_ge(sd_ready, j + 1)
                    link(dve.reciprocal(rsd[:, :], sd[:, :]))
                    link(dve.tensor_tensor(rg[:, :], cen[:, j % 2, :], rsd[:, :], ALU.mult))
                    dve.wait_ge(silu_ready, j + 1)
                    if j >= 1:
                        wait_misc(dve, ("retY", j - 1))
                    dve.tensor_tensor(rg2[:, :], rg[:, :], pair(silu, j), ALU.mult).then_inc(rg_ready, 1)
                elif kind == "ff" and arg[1] == 0:
                    j, _, m = arg
                    dve.wait_ge(hid_ps, ffn_no[arg] + 1)
                    dve.wait_ge(gateA_ready, KT * j + m + 1)
                    if m == 0 and j >= 2:
                        dve.wait_ge(hid_ps, ffn_no[(j - 2, 1, 1)] + 1)
                    elif m == 0 and j == 0:
                        dve.wait_ge(scores, UNITS * (STEP_OF[RET, 0] + 1))
                    dve.scalar_tensor_tensor(hid[0][:, j % 2, m, :], ffn_ps(arg)[:, 2 * S:4 * S], col("s2", m),
                                             gateA[:, m % 2, :], ALU.mult, ALU.mult).then_inc(hid_ready[0], 1)
                elif kind == "ffY":
                    j, = arg
                    bank = ready(item)
                    dve.tensor_tensor(ysc[:, :, :], bank[:, 0:2 * D].rearrange("p (e d) -> p e d", e=2),
                                      bcast(row("s3"), 2), ALU.mult).then_inc(y_free, 1)
                    dve.wait_ge(y_free, j + 1)
                    dve.wait_ge(x_ready, norm_no(4, j) + 1)
                    stats(5, (2 * j, 2 * j + 1), dve.tensor_tensor(Z[:, 2 * j:2 * j + 2, :], ysc[:, :, :],
                                                                   X[:, 2 * j:2 * j + 2, :], ALU.add))
                elif kind == "retY":
                    j, = arg
                    bank = ready(item)
                    add_pair(4, j, bank)

            for j in (0, 1):
                dve.memset(bd[:, 2 * j:2 * j + 2, :, :], 0.0).then_inc(zeroed_bd[j], 1)
            dve.wait_ge(ld["cols"], 16)
            dve.tensor_scalar(bqs[:, 0:1], col("bq0"), SCALE, None, ALU.mult)
            dve.tensor_scalar(bqs[:, 1:2], col("bq1"), SCALE, None, ALU.mult).then_inc(consts, 1)
            dve.tensor_scalar(mwd[:, :], cols[:, COLS["mw"] + 1:COLS["mw"] + 1 + TAPS], col("mw"), None,
                              ALU.subtract).then_inc(consts, 1)
            for item in PROLOGUE:
                run(item)
            row_max(0)
            row_max(1)
            for k, v, items in walk():
                u = UNITS * k + v
                if k == 0 and v == 1:
                    dve.wait_ge(ld["maskI"], 16)
                    dve.tensor_scalar(maskHi[:, :, :], maskI[:, :, :], -1.0, MASK_HI, ALU.add, ALU.mult)
                    dve.tensor_scalar(maskLo[:, :, :], maskI[:, :, :], -1.0, MASK_LO, ALU.add, ALU.mult).then_inc(masks, 1)
                if u + 2 < SOFTMAX_UNITS:
                    row_max(u + 2)
                elif SOFTMAX_UNITS <= u + 1 < LAST:
                    if u + 1 == SOFTMAX_UNITS:
                        take_weights(u)
                    decay(u + 1)
                if u < SOFTMAX_UNITS - 1:
                    take_weights(u)
                for item in items:
                    run(item)

        @block.tensor
        def _(pe):
            def use(item, n=0):
                bank, i, before = misc(item, n)
                if before:
                    pe.wait_ge(*reader[misc_at[item] + n - 2])
                return bank, misc_ready[i]

            def unit_scores(u):
                core, b, g, e = unit(u)
                n = u // GROUPS
                if 3 <= u < SOFTMAX_UNITS:
                    pe.wait_ge(probs_ready, u - 2)
                elif SOFTMAX_UNITS <= u < SOFTMAX_UNITS + 2:
                    pe.wait_ge(probs_ready, SOFTMAX_UNITS)
                elif u > SOFTMAX_UNITS:
                    pe.wait_ge(wT, u - 1)
                if g == 0:
                    pe.wait_ge(stat_ready, n + 1)
                if e == 0:
                    pe.wait_ge(bd_ready[b // 2][g], 16 * HG * (core + 1))
                out = scores_ps(u)
                if core == A0:
                    if u == 0:
                        pe.wait_ge(ld["bfc"], 16)
                    pe.matmul(out, bfc[:, 0, :], bcast(bfc[:, 1, :], HG), start=True, stop=False)
                elif core == A1:
                    if u == UNITS * STEP_OF[A1, 0]:
                        pe.wait_ge(masks, 1)
                    pe.matmul(out, bfc[:, 2, :], bcast(maskHi[:, b, :], HG), start=True, stop=False)
                    pe.matmul(out, bfc[:, 2, :], bcast(maskLo[:, b, :], HG), start=False, stop=False)
                pe.matmul(out, stat[:, e, :], bd[:, b, HG * g:HG * (g + 1), :].rearrange("p h s -> p (h s)"),
                          start=(core == RET), stop=True).then_inc(scores, 1)

            def unit_transposes(u):
                pe.wait_ge(probs_ready, u + 1)
                if u >= 1:
                    pe.wait_ge(wT, u)
                for i in range(HG):
                    last = pe.transpose(probsT_ps[:, S * i:S * (i + 1)], probs[:, u % 3, S * i:S * (i + 1)], ident[:, :])
                last.then_inc(probsT, 1)

            def unit_pv(u):
                n, g, e = u // GROUPS, u % GROUPS, (u // GROUPS) % 2
                pe.wait_ge(wT, u + 1)
                if g == 0:
                    pe.wait_ge(vpad_ready, n + 1)
                    if n >= 2:
                        pe.wait_ge(out_taken, n - 1)
                for i in range(HG):
                    block = slice(COLG * i, COLG * (i + 1))
                    last = pe.matmul(out_ps[e][block, :], vpad[:, e, head_of(g, i), :], weightsT[:, u % 3, i, :],
                                     start=(g == 0), stop=(g == GROUPS - 1), tile_position=(0, COLG * i))
                last.then_inc(pv, 1)

            def run(item):
                kind, arg = item[0], item[1:]
                if kind in ("projK", "projQ0", "projV"):
                    c, h = arg if kind != "projQ0" else (0, *arg)
                    src = xT0 if c == 0 else ctxT
                    pe.wait_ge(ld["xT0" if c == 0 else "ctxT"], 16)
                    pe.wait_ge(ld[("w0", "w1", "wr")[c]], 16)
                    w = (w0, w1, wr)[c]
                    bank, rd = use(item)
                    if kind == "projV":
                        for b in range(4 * h, 4 * h + 4):
                            last = pe.matmul(bank[:, D * (b % 4):D * (b % 4 + 1)], src[:, S * b:S * (b + 1)],
                                             w[:, 2 if c != RET else 4, :], start=True, stop=True)
                    else:
                        last = pe.matmul(bank, w[:, 1 if kind == "projQ0" else 0, :], src[:, 512 * h:512 * (h + 1)],
                                         start=True, stop=True)
                    last.then_inc(rd, 1)
                elif kind == "projK4":
                    h, = arg
                    for n in range(2):
                        bank, rd = use(item, n)
                        pe.wait_ge(ld["wr"], 16)
                        pe.matmul(bank, wr[:, 2 + n, :], ctxT[:, 512 * h:512 * (h + 1)], start=True, stop=True).then_inc(rd, 1)
                elif kind == "projQ1":
                    j, = arg
                    bank, rd = use(item)
                    pe.wait_ge(xTs_ready, xT_no(0, j) + 1)
                    pe.matmul(bank[:, 0:2 * S], w1[:, 1, :], xTs[:, 0, :], start=True, stop=True).then_inc(rd, 1)
                elif kind == "rT":
                    c, b = arg
                    bank, rd = use(item)
                    pe.wait_ge(rexp_ready, seq_no(c, b) + 1)
                    pe.transpose(bank[:, 0:S], rexp[:, b % 2, :, :].rearrange("p h d -> p (h d)"), ident[:, :]).then_inc(rd, 1)
                elif kind == "y":
                    c, b = arg
                    bank, rd = use(item)
                    pe.wait_ge(out_taken, seq_no(c, b) + 1)
                    pe.matmul(bank[:, 0:D], outT[:, b % 2, :], (w0, w1)[c][:, 3, :], start=True, stop=True).then_inc(rd, 1)
                elif kind == "xT":
                    n, j = arg
                    bank, rd = use(item)
                    pe.wait_ge(x_ready, norm_no(n, j) + 1)
                    for e in range(2):
                        last = pe.transpose(bank[:, S * e:S * (e + 1)], X[:, 2 * j + e, :], ident[:, :])
                    last.then_inc(rd, 1)
                elif kind == "route":
                    j, = arg
                    bank, rd = use(item)
                    pe.wait_ge(ld["wm"], 16)
                    pe.wait_ge(xTs_ready, xT_no(1, j) + 1)
                    N = 128 + E_
                    for e in range(2):
                        last = pe.matmul(bank[:, N * e:N * (e + 1)], xTs[:, 1, S * e:S * (e + 1)], wm[:, 256:256 + N],
                                         start=True, stop=True)
                    last.then_inc(rd, 1)
                elif kind == "gatedT":
                    j, = arg
                    bank, rd = use(item)
                    pe.wait_ge(gated_ready, j + 1)
                    for e in range(2):
                        last = pe.transpose(bank[:, S * e:S * (e + 1)], gated[:, e, :, :].rearrange("p a b -> p (a b)"), ident[:, :])
                    last.then_inc(rd, 1)
                elif kind == "experts":
                    j, = arg
                    bank, rd = use(item)
                    pe.wait_ge(gatedT_ready, j + 1)
                    for e in range(2):
                        pe.matmul(bank[:, D * e:D * (e + 1)], xTs[:, 1, S * e:S * (e + 1)], wm[:, 0:128], start=True, stop=False)
                        last = pe.matmul(bank[:, D * e:D * (e + 1)], gatedT[:, S * e:S * (e + 1)], wm[:, 128:256],
                                         start=False, stop=True)
                    last.then_inc(rd, 1)
                elif kind == "projP":
                    j, = arg
                    bank, rd = use(item)
                    pe.wait_ge(ld["wf"], 16)
                    pe.wait_ge(xTs_ready, xT_no(2, j) + 1)
                    pe.matmul(bank[:, 0:2 * S], wf[:, 0, :], xTs[:, 2, :], start=True, stop=True).then_inc(rd, 1)
                elif kind == "taps":
                    j, c = arg
                    if c == 0:
                        pe.wait_ge(tapW_ready, 2)
                        pe.wait_ge(p_ready, j + 1)
                    bank, rd = use(item)
                    chunk = split_taps(DVE_TAPS, PE_TAPS, c)
                    for i in split_taps(DVE_TAPS, PE_TAPS, c):
                        last = pe.matmul(bank[:, 0:2 * S], tapW[:, i - DVE_TAPS, :],
                                         pPad[:, j % 2, :, TAPS - 1 - i:TAPS - 1 - i + S],
                                         start=(i == chunk[0]), stop=(i == chunk[-1]))
                    last.then_inc(rd, 1)
                elif kind == "memY":
                    j, = arg
                    bank, rd = use(item)
                    pe.wait_ge(taps_done, TAPS_DONE * (j + 1))
                    pe.wait_ge(pool_taps, POOL_TAPS * (j + 1))
                    for e in range(2):
                        pe.matmul(bank[:, D * e:D * (e + 1)], mem[:, j % 2, e, :], wf[:, 1, :], start=True, stop=False)
                        last = pe.matmul(bank[:, D * e:D * (e + 1)], memP[:, j % 2, e, :], wf[:, 1, :], start=False, stop=True)
                    last.then_inc(rd, 1)
                elif kind == "projQ4":
                    j, = arg
                    for n in range(2):
                        bank, rd = use(item, n)
                        pe.wait_ge(xTs_ready, xT_no(3, j) + 1)
                        pe.matmul(bank[:, 0:2 * S], wr[:, n, :], xTs[:, 3, :], start=True, stop=True).then_inc(rd, 1)
                elif kind == "silu":
                    j, = arg
                    bank, rd = use(item)
                    pe.matmul(bank[:, 0:2 * S], wr[:, 5, :], xTs[:, 3, :], start=True, stop=True).then_inc(rd, 1)
                elif kind == "center":
                    j, = arg
                    bank, rd = use(item)
                    pe.wait_ge(ld["mats"], 16)
                    pe.wait_ge(out_taken, 2 * B + 2 * j + 2)
                    pe.matmul(bank[:, 0:2 * S], mats[:, 1, :], ret[:, j % 2, :], start=True, stop=True).then_inc(rd, 1)
                elif kind == "spread":
                    j, = arg
                    bank, rd = use(item)
                    pe.wait_ge(sq_ready, j + 1)
                    pe.matmul(bank[:, 0:2 * S], mats[:, 0, :], sq[:, :], start=True, stop=True).then_inc(rd, 1)
                elif kind == "retY":
                    j, = arg
                    bank, rd = use(item)
                    pe.wait_ge(rg_ready, j + 1)
                    for e in range(2):
                        last = pe.matmul(bank[:, D * e:D * (e + 1)], rg2[:, S * e:S * (e + 1)], wr[:, 6, :], start=True, stop=True)
                    last.then_inc(rd, 1)

                elif kind == "ff":
                    j, layer, m = arg
                    n = ffn_no[arg]
                    if n == 0:
                        pe.wait_ge(ld["wi"], 16)
                    if ffn_before[n]:
                        pe.wait_ge(*hid_reader(ffn_before[n]))
                    elif ffn_at[n] in (2, 3):
                        pe.wait_ge(wT, SOFTMAX_UNITS)
                    elif ffn_at[n] in (0, 1):
                        pe.wait_ge(wT, LAST)
                    else:
                        pe.wait_ge(out_taken, 3 * B)
                    bank = ffn_ps(arg)
                    if layer == 0:
                        pe.wait_ge(xTs_ready, xT_no(4, j) + 1)
                        for i in range(2):
                            last = pe.matmul(bank[:, 2 * S * i:2 * S * (i + 1)], wi[:, i, 128 * m:128 * (m + 1)],
                                             x5T[:, j, :], start=True, stop=True)
                    else:
                        if layer == 1 and j == 0:
                            pe.wait_ge(ld["wh"], 16)
                        pe.wait_ge(hid_ready[layer - 1], KT * (j + 1) if layer == 1 else 2 * (j + 1))
                        for half in range(2):
                            o = 128 * (2 * m + half)
                            for c in range(KT):
                                last = pe.matmul(bank[:, 2 * S * half:2 * S * (half + 1)], wh[:, layer - 1, c, o:o + 128],
                                                 hid[layer - 1][:, j % 2, c, :], start=(c == 0), stop=(c == KT - 1))
                    last.then_inc(hid_ps, 1)
                elif kind == "ffY":
                    j, = arg
                    bank, rd = use(item)
                    if j == 0:
                        pe.wait_ge(ld["wo3"], 16)
                    pe.wait_ge(hid_ready[2], 2 * (j + 1))
                    for e in range(2):
                        for c in range(KT):
                            last = pe.matmul(bank[:, D * e:D * (e + 1)], hid[2][:, j % 2, c, S * e:S * (e + 1)],
                                             wo3[:, c, :], start=(c == 0), stop=(c == KT - 1))
                    last.then_inc(rd, 1)

            for item in PROLOGUE:
                run(item)
            pe.wait_ge(ld["ident"], 16)
            unit_scores(0)
            unit_scores(1)
            for k, v, items in walk():
                u = UNITS * k + v
                if u + 2 < SOFTMAX_UNITS:
                    unit_scores(u + 2)
                elif SOFTMAX_UNITS <= u + 1 < LAST:
                    unit_scores(u + 1)
                if u < SOFTMAX_UNITS:
                    unit_transposes(u)
                if 1 <= u <= LAST:
                    unit_pv(u - 1)
                for item in items:
                    run(item)


_IN = {"float32": F32, "bfloat16": BF16, "int32": I32}


def shape_constants():
    import numpy as np

    f = np.float32
    eye = np.eye(128, dtype=f)
    group = np.kron(np.eye(H, dtype=f), np.full((DH, DH), 1 / DH, f))
    mats = np.stack([group, eye - group], 1)
    pos = np.arange(S)
    bfc = np.stack([-1e10 * eye, (pos[None, :] > pos[:, None]).astype(f), MASK_DIAG * eye], 1).astype(mybir.dt.np(BF16))
    half = DH // 2
    base = ((np.arange(0, DH, 2, dtype=f) + f(0.4 * DH)) / f(1.4 * DH)).astype(f)
    power = (np.arange(-(S // 2), -(S // 2) + S, dtype=f) / f(512.0))[:, None]
    scale = (base[None, :] ** power).astype(f)
    inv_freq = (f(1.0) / f(10000.0) ** (np.arange(half, dtype=f) / f(half))).astype(f)
    ang = (np.arange(S, dtype=f)[:, None] * inv_freq[None, :]).astype(f)
    sin, cos = np.sin(ang), np.cos(ang)
    sign = np.tile(np.array([-1, 1], f), half)
    tables = []
    for s_ in (scale, f(1.0) / scale):
        tables.append(np.repeat(cos * s_, 2, axis=-1))
        tables.append(np.repeat(sin * s_, 2, axis=-1) * sign)
    xpos = np.stack([np.tile(a.T, (H, 1)) for a in tables], 1)
    gammas = (1.0 - np.exp(np.linspace(np.log(1 / 32), np.log(1 / 512), H, dtype=f))).astype(f)
    growth = np.repeat(gammas.astype(np.float64), DH)[:, None] ** (pos - S // 2)[None, :]
    xpos = (xpos * np.stack([growth, growth, 1 / growth, 1 / growth], 1)).astype(f)
    causal = (pos[:, None] <= pos[None, :]).astype(f)
    return dict(ident=eye, mats=mats, bfc=bfc, xpos=xpos, causalT=causal)


def lay_out(i):
    import numpy as np

    def blocks(w):
        return w.reshape(-1, 128, w.shape[-1]).transpose(1, 0, 2)

    def heads(w):
        return w.transpose(1, 0, 2).reshape(D, D)

    def swapped(w):
        return w.reshape(D, -1, 2)[:, :, ::-1].reshape(D, D)

    features = lambda x: x.transpose(2, 0, 1).reshape(D, B * S)
    column = lambda v: v.reshape(-1, 128).T
    wq, wk, wv = (heads(i[f"L1_xattn_W_{n}"]) for n in "QKV")
    a = {
        "X": i["x"].transpose(1, 0, 2),
        "xT0": features(i["x"]),
        "ctxT": features(i["ctx_1024"]),
        "gT": i["fside_BxSxS2_0"].transpose(2, 0, 1),
        "maskI": i["mask_BxSxS2_ik1"].transpose(1, 0, 2),
        "w0": np.stack([i[f"L0_attn_W{n}"].T for n in "kqvo"], 1),
        "w1": np.stack([i[f"L0_xattn_w{n}_k"] for n in "kqvo"], 1),
        "wr": np.stack([wq, swapped(wq), wk, swapped(wk), wv, i["L1_xattn_g_w"].T, i["L1_xattn_out_w"].T], 1),
        "wm": np.concatenate([i["L0_ffn_base_w"].T, i["L0_ffn_lora_B"].reshape(E_ * R_, D),
                              i["L0_ffn_lora_A"].transpose(1, 0, 2).reshape(D, E_ * R_), i["L0_ffn_router_w"].T], 1),
        "wf": np.stack([i["L1_attn_W1"], i["L1_attn_W2"]], 1),
        "wi": np.stack([i["L1_ffn_w1_w"].T, i["L1_ffn_w2_w"].T], 1),
        "wh": np.stack([blocks(i["L1_ffn_h1_w"].T), blocks(i["L1_ffn_h2_w"].T)], 1),
        "wo3": blocks(i["L1_ffn_w3_w"].T),
        "cols": np.concatenate([column(i[n]) for n in (
            "L0_attn_bq", "L0_attn_bk", "L0_xattn_wq_b", "L0_xattn_wk_b", "L1_attn_bias1", "L1_xattn_g_b", "L1_ffn_w1_s",
            "L1_ffn_w2_s", "L1_ffn_h1_s", "L1_ffn_h2_s")] + [i["L1_attn_memory_weights"].T], 1),
        "rows": np.broadcast_to(np.stack([i[n] for n in (
            "L0_attn_bv", "L0_attn_bo", "L0_xattn_wv_b", "L0_xattn_wo_b", "L0_ffn_base_b", "L1_attn_bias2", "L1_xattn_out_b",
            "L1_ffn_w3_s")]), (128, len(ROWS), 128)),
        "rbr": np.broadcast_to(i["L0_ffn_router_b"], (128, E_)),
    }
    return {name: np.ascontiguousarray(v) for name, v in a.items()}


def kernel(**inputs):
    import numpy as np
    import concourse.bacc as bacc
    from concourse.bass_utils import run_bass_kernel_spmd

    nc = bacc.Bacc("TRN2", target_bir_lowering=False, num_devices=1)
    arrays = lay_out({name: np.asarray(a) for name, a in inputs.items()}) | shape_constants()
    t = {name: nc.dram_tensor(f"in_{name}", a.shape, _IN[a.dtype.name], kind="ExternalInput").ap()
         for name, a in arrays.items()}
    t["out"] = nc.dram_tensor("out", (128, B, D), F32, kind="ExternalOutput").ap()
    build(nc, t)
    r = run_bass_kernel_spmd(nc, [{f"in_{name}": a for name, a in arrays.items()}], core_ids=[0])
    return np.ascontiguousarray(r.results[0]["out"].transpose(1, 0, 2))
```
